# Optimizing a Trainium2 kernel written in Bass

```python
import numpy as np
import jax
import jax.numpy as jnp

def _softmax(x, axis=-1):
    return jax.nn.softmax(x, axis=axis)

def _gelu(x):
    return jax.nn.gelu(x, approximate=True)

def _silu(x):
    return jax.nn.silu(x)

def _sigmoid(x):
    return jax.nn.sigmoid(x)

def _layernorm(x, axis=-1, eps=1e-05):
    m = jnp.mean(x, axis=axis, keepdims=True)
    v = jnp.var(x, axis=axis, keepdims=True)
    return (x - m) / jnp.sqrt(v + eps)

def _scatter_add(tgt, idx, src, axis=0):
    return tgt.at[idx].add(src)

def _segment_sum(src, seg, n):
    return jax.ops.segment_sum(src, seg, n)
kernel_name = 'mk_seq_postln_d1_jaxref_r8_f57cc1'

def setup_inputs(seed: int=0):
    np.random.seed(seed)
    _w = jnp.asarray

    def _L0_attn_setup():
        import jax, jax.numpy as jnp
        import numpy as np
        B, T, H, S, F, G = (2, 256, 512, 128, 1248, 6)
        GRAD_ORDER_MIN = 4
        THD = 2.5
        key = jax.random.key(seed)
        ks = jax.random.split(key, 9)
        sc = 0.02
        hidden_states = jax.random.normal(ks[0], (B, T, H), jnp.float32)
        up_w = jax.random.normal(ks[1], (S, H), jnp.float32) * sc
        gate_w = jax.random.normal(ks[2], (S, H), jnp.float32) / np.sqrt(H)
        local_point = jax.random.normal(ks[3], (S,), jnp.float32)
        local_approx_output = jax.random.normal(ks[4], (H, S), jnp.float32) * sc
        fuse_weight = jax.random.normal(ks[5], (H, S, G), jnp.float32) * sc
        discount_factor = jnp.asarray(np.cumsum(np.log(np.arange(1, G + 1, dtype=np.float64))), jnp.float32)
        ffn_gate_w = jax.random.normal(ks[6], (F, H), jnp.float32) * sc
        ffn_up_w = jax.random.normal(ks[7], (F, H), jnp.float32) * sc
        ffn_down_w = jax.random.normal(ks[8], (H, F), jnp.float32) * sc
        return {'hidden_states': hidden_states, 'up_w': up_w, 'gate_w': gate_w, 'local_point': local_point, 'local_approx_output': local_approx_output, 'fuse_weight': fuse_weight, 'discount_factor': discount_factor, 'ffn_gate_w': ffn_gate_w, 'ffn_up_w': ffn_up_w, 'ffn_down_w': ffn_down_w}
    _L0_attn_in = _L0_attn_setup()

    def _L0_ffn_setup():
        import jax, jax.numpy as jnp
        import numpy as np
        NF4_CODE = jnp.array([-1.0, -0.6961928009986877, -0.5250730514526367, -0.39491748809814453, -0.28444138169288635, -0.18477343022823334, -0.09105003625154495, 0.0, 0.07958029955625534, 0.16093020141124725, 0.24611230194568634, 0.33791524171829224, 0.44070982933044434, 0.5626170039176941, 0.7229568362236023, 1.0], dtype=jnp.float32)
        BLOCKSIZE = 64

        def nf4_quant_dequant(w):
            shape = w.shape
            flat = w.reshape(-1, BLOCKSIZE)
            absmax = jnp.max(jnp.abs(flat), axis=1, keepdims=True)
            normalized = flat / jnp.where(absmax == 0, 1.0, absmax)
            bounds = (NF4_CODE[:-1] + NF4_CODE[1:]) * 0.5
            idx = jnp.searchsorted(bounds, normalized)
            return (NF4_CODE[idx] * absmax).reshape(shape)
        key = jax.random.key(seed)
        k1, k2, k3, kx = jax.random.split(key, 4)
        D, H = (512, 1376)
        scale = 0.02
        w1 = jax.random.normal(k1, (H, D), jnp.float32) * scale
        w2 = jax.random.normal(k2, (H, D), jnp.float32) * scale
        w3 = jax.random.normal(k3, (D, H), jnp.float32) * scale
        x = jax.random.normal(kx, (2, 256, D), jnp.float32)
        return {'x': x, 'w1': w1, 'w2': w2, 'w3': w3}
    _L0_ffn_in = _L0_ffn_setup()
    _d = {'L0_attn_hidden_states': _L0_attn_in['hidden_states'], 'L0_attn_up_w': _L0_attn_in['up_w'], 'L0_attn_gate_w': _L0_attn_in['gate_w'], 'L0_attn_local_point': _L0_attn_in['local_point'], 'L0_attn_local_approx_output': _L0_attn_in['local_approx_output'], 'L0_attn_fuse_weight': _L0_attn_in['fuse_weight'], 'L0_attn_discount_factor': _L0_attn_in['discount_factor'], 'L0_attn_ffn_gate_w': _L0_attn_in['ffn_gate_w'], 'L0_attn_ffn_up_w': _L0_attn_in['ffn_up_w'], 'L0_attn_ffn_down_w': _L0_attn_in['ffn_down_w'], 'L0_ffn_w1': _L0_ffn_in['w1'], 'L0_ffn_w2': _L0_ffn_in['w2'], 'L0_ffn_w3': _L0_ffn_in['w3']}
    _x0 = _d['L0_attn_hidden_states']
    _d['L0_attn_hidden_states'] = jax.random.normal(jax.random.fold_in(jax.random.key(seed), 1), (2, 512, 512), dtype=_x0.dtype)
    del _x0
    return _d

def reference(L0_attn_hidden_states, L0_attn_up_w, L0_attn_gate_w, L0_attn_local_point, L0_attn_local_approx_output, L0_attn_fuse_weight, L0_attn_discount_factor, L0_attn_ffn_gate_w, L0_attn_ffn_up_w, L0_attn_ffn_down_w, L0_ffn_w1, L0_ffn_w2, L0_ffn_w3):

    def _L0_attn_ref(hidden_states, up_w, gate_w, local_point, local_approx_output, fuse_weight, discount_factor, ffn_gate_w, ffn_up_w, ffn_down_w):
        import jax, jax.numpy as jnp
        import numpy as np
        B, T, H, S, F, G = (2, 256, 512, 128, 1248, 6)
        GRAD_ORDER_MIN = 4
        THD = 2.5
        approx_up = hidden_states @ up_w.T
        gate_pre = hidden_states @ gate_w.T
        delta = gate_pre - local_point
        neg_factor = jnp.where(delta > 0, 1.0, -1.0).astype(hidden_states.dtype)
        delta_abs = jnp.abs(delta)
        log_delta = jnp.log(delta_abs)
        keep = (delta_abs <= THD).astype(hidden_states.dtype)
        approx_out = approx_up @ local_approx_output.T
        for idx in range(G):
            m = idx + 1
            dterm = jnp.exp(log_delta * m - discount_factor[idx])
            if m % 2 == 1:
                dterm = dterm * neg_factor
            tmp = dterm * approx_up
            if m > GRAD_ORDER_MIN:
                tmp = tmp * keep
            approx_out = approx_out + tmp @ fuse_weight[:, :, idx].T
        ffn_out = jax.nn.silu(hidden_states @ ffn_gate_w.T) * (hidden_states @ ffn_up_w.T) @ ffn_down_w.T
        return approx_out + ffn_out

    def _L0_ffn_ref(x, w1, w2, w3):
        import jax, jax.numpy as jnp
        import numpy as np
        NF4_CODE = jnp.array([-1.0, -0.6961928009986877, -0.5250730514526367, -0.39491748809814453, -0.28444138169288635, -0.18477343022823334, -0.09105003625154495, 0.0, 0.07958029955625534, 0.16093020141124725, 0.24611230194568634, 0.33791524171829224, 0.44070982933044434, 0.5626170039176941, 0.7229568362236023, 1.0], dtype=jnp.float32)
        BLOCKSIZE = 64

        def nf4_quant_dequant(w):
            shape = w.shape
            flat = w.reshape(-1, BLOCKSIZE)
            absmax = jnp.max(jnp.abs(flat), axis=1, keepdims=True)
            normalized = flat / jnp.where(absmax == 0, 1.0, absmax)
            bounds = (NF4_CODE[:-1] + NF4_CODE[1:]) * 0.5
            idx = jnp.searchsorted(bounds, normalized)
            return (NF4_CODE[idx] * absmax).reshape(shape)
        dq1 = nf4_quant_dequant(w1)
        dq2 = nf4_quant_dequant(w2)
        dq3 = nf4_quant_dequant(w3)
        gate = jnp.einsum('bsd,hd->bsh', x, dq1)
        up = jnp.einsum('bsd,hd->bsh', x, dq2)
        h = jax.nn.silu(gate) * up
        return jnp.einsum('bsh,dh->bsd', h, dq3)
    x = L0_attn_hidden_states
    x = _layernorm(x + _L0_attn_ref(x, L0_attn_up_w, L0_attn_gate_w, L0_attn_local_point, L0_attn_local_approx_output, L0_attn_fuse_weight, L0_attn_discount_factor, L0_attn_ffn_gate_w, L0_attn_ffn_up_w, L0_attn_ffn_down_w), axis=-1)
    x = _layernorm(x + _L0_ffn_ref(x, L0_ffn_w1, L0_ffn_w2, L0_ffn_w3), axis=-1)
    return x

_drawn_inputs = setup_inputs


def setup_inputs(seed=0):
    import zlib

    import numpy as np

    out = dict(_drawn_inputs(seed))
    spreads = {}
    factors = {}
    for name, (base, spread) in spreads.items():
        noise = np.random.default_rng([zlib.crc32(name.encode()), seed]).standard_normal(out[name].shape)
        drawn = base * np.exp(spread * noise) if base else spread * noise
        out[name] = jnp.asarray(drawn.astype(out[name].dtype))
    for name, factor in factors.items():
        out[name] = (out[name] * factor).astype(out[name].dtype)
    return out
```

```python
from contextlib import ExitStack

import numpy as np
import concourse.bass as bass
from concourse import mybir

F32 = mybir.dt.float32
F32R = mybir.dt.float32r
BF16 = mybir.dt.bfloat16
ALU = mybir.AluOpType
ACT = mybir.ActivationFunctionType
AX_X = mybir.AxisListType.X

P = 128
TOK = 1024
D = 512
DC = D // P
HALF = 512
TT = TOK // P
S = 128
G = 6
F1 = 1248
F2 = 1376
C1 = -(-F1 // P)
C2 = -(-F2 // P)
KEEP_FROM = 5
THD = 2.5
EPS = 1e-5
BLOCK = 64
TINY = 1.1754943508222875e-38

CODE = np.array([-1.0, -0.6961928009986877, -0.5250730514526367, -0.39491748809814453, -0.28444138169288635,
                 -0.18477343022823334, -0.09105003625154495, 0.0, 0.07958029955625534, 0.16093020141124725,
                 0.24611230194568634, 0.33791524171829224, 0.44070982933044434, 0.5626170039176941,
                 0.7229568362236023, 1.0], dtype=np.float32)
BOUND = (CODE[:-1] + CODE[1:]) * np.float32(0.5)
NB = len(BOUND)
STEEP = 2.0 ** 60


def code_rises():
    rises = []
    for k in range(NB):
        r = np.float32(CODE[k + 1] - CODE[k])
        near = (r, np.nextafter(r, np.float32(2)), np.nextafter(r, np.float32(0)))
        rises.append(float([x for x in near if np.float32(CODE[k] + x) == CODE[k + 1]][0]))
    return rises


RISE = code_rises()

UW = 1024
PAIR = 2 * F2
W3_UNITS = [(q, a, min(UW, PAIR - a)) for q in range(2) for a in range(0, PAIR, UW)]
UNITS = C2 + len(W3_UNITS)


def unit_shape(u):
    if u < C2:
        return u, min(P, F2 - u * P), UW
    q, a, width = W3_UNITS[u - C2]
    return 3 * q + a // UW, P, width


STEPS = [(u, k) for _, u, k in sorted((NB * u + 1.8 * k, u, k) for u in range(UNITS) for k in range(NB))]
FIRST = {u: STEPS.index((u, 0)) for u in range(UNITS)}
LAST = {u: STEPS.index((u, NB - 1)) for u in range(UNITS)}
PREP = {u: max(0, FIRST[u] - 8) for u in range(UNITS)}
PREPS = {s: [u for u in range(UNITS) if PREP[u] == s] for s in range(len(STEPS))}

TERM_STEPS, PAIR_STEPS, DOWN_STEPS, FFN_STEPS = 3, 4.25, 4, 5


def deal():
    done, plan = 0, {}

    def give(key, upto):
        nonlocal done
        upto = min(len(STEPS), max(done, int(upto)))
        plan[key] = (done, upto)
        done = upto

    for m in range(G + 1):
        give(("term", m), done + TERM_STEPS)
    base = done
    for i in range(2 * C1):
        give(("pair", 1, i), base + PAIR_STEPS * (i + 1))
    for f in range(C1):
        give(("down", 1, f), done + DOWN_STEPS)
    give(("norm", 1), max(done, LAST[0] + 1))
    base = done
    for i in range(2 * C2):
        f = i // 2
        need = LAST[min(f + 1, C2 - 1)] + 1 if i % 2 == 0 else 0
        most = PREP[C2] if i < 3 else PREP[C2 + 3] if i < 9 else len(STEPS)
        give(("pair", 2, i), min(max(base + FFN_STEPS * (i + 1), need), most))
    give(("w3", 0), LAST[C2 + 2] + 1)
    give(("w3", 1), len(STEPS))
    return plan


PLAN = deal()

JOBS = ([("pre", 0)] + [("fuse", m) for m in range(G + 1)] + [("in", f) for f in range(C1)]
        + [("out", f) for f in range(C1)] + [("nf4in", f) for f in range(C2)] + [("nf4out", f) for f in range(C2)])
JOB = {job: j for j, job in enumerate(JOBS)}
RAW_JOBS = 1 + (G + 1) + 2 * C1
RAW_SLOTS = 5
LHS = {("fuse", m): m for m in range(G + 1)}
LHS.update({("out", f): G + 1 + f for f in range(C1)})
LHS.update({("nf4out", f): G + 1 + C1 + f for f in range(C2)})


def rows(f, width):
    return min(P, width - f * P)


def build(nc, xT, xN, w_pre, w_fuse, w_in, w_out, point, discount, w1, w2, w3, ident_in, out):
    with ExitStack() as ctx:
        def sb(name, shape, dt=F32):
            return ctx.enter_context(nc.sbuf_tensor(name, shape, dt))

        def sem(name):
            return ctx.enter_context(nc.semaphore(name))

        x_hi, x_lo = sb("x_hi", [P, DC, TOK], F32R), sb("x_lo", [P, DC, TOK], F32R)
        R = sb("R", [P, TT, D])
        h = sb("h", [P, C2 * TOK])
        w_hi, w_lo = sb("w_hi", [P, 2, 1024], F32R), sb("w_lo", [P, 2, 1024], F32R)
        l_hi, l_lo = sb("l_hi", [P, 2, TOK], F32R), sb("l_lo", [P, 2, TOK], F32R)
        w3T = sb("w3T", [P, C2 * D])
        Q = sb("Q", [P, C2, UW])
        acc = sb("acc", [P, 2, UW])
        NR = 3
        relu = sb("relu", [P, NR, UW], BF16)
        amax, rcp = sb("amax", [P, UNITS, UW // BLOCK]), sb("rcp", [P, UNITS, UW // BLOCK])
        ident = sb("ident", [P, P])
        point_sb, disc, fact = sb("point_sb", [P, 1]), sb("disc", [P, G]), sb("fact", [P, G])
        stats, mv = sb("stats", [P, TT, 6]), sb("mv", [P, TT, 2])
        std = sb("std", [P, 5, TT])
        PS = ctx.enter_context(nc.psum_tensor("PS", [P, 8, 512], F32))

        xT_raw = h[:, 0:DC * TOK].rearrange("p (c t) -> p c t", c=DC)
        up, delta, ta, tb, kept = (h[:, (DC + i) * TOK:(DC + i + 1) * TOK] for i in range(5))
        term_tile = [up, ta, tb, ta, tb, ta, tb]

        def w_raw(j):
            return w3T[:, (j % RAW_SLOTS) * 1024:(j % RAW_SLOTS) * 1024 + 1024]

        def job_shape(j):
            kind, f = JOBS[j]
            if kind in ("pre",):
                return P, 2 * DC * P
            if kind == "fuse":
                return P, D
            if kind == "in":
                return P, 2 * DC * rows(f, F1)
            if kind == "nf4in":
                return P, 2 * DC * rows(f, F2)
            return rows(f, F1 if kind == "out" else F2), D

        s_point = sem("s_point")
        s_ident = sem("s_ident")
        s_x = [sem(f"s_x{c}") for c in range(DC)]
        s_R = sem("s_R")
        s_raw = [sem(f"s_raw{i}") for i in range(RAW_SLOTS)]
        s_q = [sem(f"s_q{i}") for i in range(C2)]
        s_out = sem("s_out")
        s_fact = sem("s_fact")
        s_xh, s_xl = sem("s_xh"), sem("s_xl")
        s_whi = sem("s_whi")
        s_wlo = sem("s_wlo")
        s_wlo4 = sem("s_wlo4")
        s_lhi = sem("s_lhi")
        s_llo_t = sem("s_llo_t")
        s_llo_h = sem("s_llo_h")
        s_pre = sem("s_pre")
        s_pre_read = sem("s_pre_read")
        s_t = sem("s_t")
        s_keep = sem("s_keep")
        s_pair = sem("s_pair")
        s_silu = sem("s_silu")
        s_h = sem("s_h")
        s_l_used = sem("s_l_used")
        s_tile = sem("s_tile")
        s_y = sem("s_y")
        s_st, s_ln, s_sqrt, s_norm = sem("s_st"), sem("s_ln"), sem("s_sqrt"), sem("s_norm")
        s_xtr = sem("s_xtr")
        s_prep = sem("s_prep")
        s_nrm = sem("s_nrm")
        s_relu = sem("s_relu")
        s_step = sem("s_step")
        s_dq = sem("s_dq")
        s_tr = sem("s_tr")
        s_w3tr = sem("s_w3tr")
        s_w3T = sem("s_w3T")

        block = ctx.enter_context(nc.Block())

        def wait_stage2(eng, n):
            lasts = [G, G + C1, G + C1 + C2]
            if n in lasts:
                eng.wait_ge(s_tile, TT * (lasts.index(n) + 1))
            else:
                eng.wait_ge(s_l_used, n + 1 - sum(1 for x in lasts if x < n))

        def wait_w_slot(eng, j):
            if j < 2:
                return
            kind, f = JOBS[j - 2]
            if kind == "pre":
                eng.wait_ge(s_pre, 1)
            elif kind in ("in", "nf4in"):
                eng.wait_ge(s_pair, 2 * (f + 1) + (2 * C1 if kind == "nf4in" else 0))
            else:
                wait_stage2(eng, LHS[JOBS[j - 2]])

        def lo_jobs_raw(j):
            return sum(1 for kind, _ in JOBS[:j + 1] if kind != "nf4in")

        def quant_view(u):
            slot, p, width = unit_shape(u)
            return Q[0:p, slot, 0:width]

        def scale_view(t, u):
            _, p, width = unit_shape(u)
            n = width // BLOCK
            return t[0:p, u, 0:n].unsqueeze(2).broadcast_to([p, n, BLOCK])

        @block.sync
        def _(sp):
            def load_job(j):
                kind, f = JOBS[j]
                if j >= RAW_SLOTS:
                    sp.wait_ge(s_wlo, j - RAW_SLOTS + 1)
                p, n = job_shape(j)
                src = {"pre": lambda: w_pre, "fuse": lambda: w_fuse[f], "in": lambda: w_in[:, f * 1024:f * 1024 + n],
                       "out": lambda: w_out[f * P:f * P + p, :]}[kind]()
                sp.dma_start(w_raw(j)[0:p, 0:n], src).then_inc(s_raw[j % RAW_SLOTS], 16)

            def load_unit(u):
                _, p, _ = unit_shape(u)
                sp.dma_start(Q[0:p, u, 0:D], w1[u * P:u * P + p, :]).then_inc(s_q[u], 16)
                sp.dma_start(Q[0:p, u, D:2 * D], w2[u * P:u * P + p, :]).then_inc(s_q[u], 16)

            load_job(0)
            for c in range(DC):
                sp.dma_start(xT_raw[:, c, :], xT[:, c, :]).then_inc(s_x[c], 16)
                if c == 0:
                    load_unit(0)
                    sp.dma_start(point_sb[:], point).then_inc(s_point, 16)
                    sp.dma_start(disc[:], discount.broadcast_to([P, G])).then_inc(s_point, 16)
            load_job(1)
            load_unit(1)
            for j in range(2, RAW_SLOTS):
                load_job(j)
            sp.dma_start(R[:], xN).then_inc(s_R, 16)
            sp.dma_start(ident[:], ident_in).then_inc(s_ident, 16)
            for u in range(2, C2):
                load_unit(u)
            for j in range(RAW_SLOTS, RAW_JOBS):
                load_job(j)
            for q in range(2):
                sp.wait_ge(s_tr, 3 * q + 3)
                sp.dma_start(Q[:, 3 * q:3 * q + 3, :].rearrange("p a n -> p (a n)")[:, 0:PAIR],
                             w3[q * P:(q + 1) * P, :]).then_inc(s_q[3 * q], 16)
            for t in range(TT):
                sp.wait_ge(s_norm, TT + t + 1)
                sp.dma_start(out[t * P:(t + 1) * P, :], R[:, t, :]).then_inc(s_out, 16)
            sp.wait_ge(s_out, 16 * TT)

        @block.scalar
        def _(act):
            def copy(dst, src, **kw):
                return nc.scalar.activation(dst, src, ACT.Copy, **kw)

            def step_functions(key):
                a, b = PLAN[key]
                for s in range(a, b):
                    u, k = STEPS[s]
                    _, p, width = unit_shape(u)
                    if k == 0:
                        act.wait_ge(s_nrm, u + 1)
                    if s >= NR:
                        act.wait_ge(s_step, s - NR + 1)
                    nc.scalar.activation(relu[0:p, s % NR, 0:width], quant_view(u), ACT.Relu, scale=STEEP,
                                         bias=float(-BOUND[k]) * STEEP).then_inc(s_relu, 1)

            def split_raw(j):
                p, n = job_shape(j)
                act.wait_ge(s_raw[j % RAW_SLOTS], 16 * (j // RAW_SLOTS + 1))
                wait_w_slot(act, j)
                copy(w_hi[0:p, j % 2, 0:n], w_raw(j)[0:p, 0:n]).then_inc(s_whi, 1)

            def split_h(job):
                kind, f = job
                p, n = rows(f, F1 if kind == "out" else F2), LHS[job]
                act.wait_ge(s_h, 2 * (f + 1) + (2 * C1 if kind == "nf4out" else 0))
                wait_stage2(act, n - 2)
                copy(l_hi[0:p, n % 2, :], h[0:p, f * TOK:(f + 1) * TOK]).then_inc(s_lhi, 1)

            def silu(i, layer):
                f, half, g = i // 2, i % 2, i + (layer - 1) * 2 * C1
                p, bank = rows(f, F1 if layer == 1 else F2), 2 * ((i + 1) % 3)
                act.wait_ge(s_pair, g + 1)
                if layer == 2 and i == 0:
                    act.wait_ge(s_llo_h, C1)
                nc.scalar.activation(h[0:p, f * TOK + half * HALF:f * TOK + (half + 1) * HALF], PS[0:p, bank, :],
                                     ACT.Silu).then_inc(s_silu, 1)

            act.wait_ge(s_point, 32)
            nc.scalar.activation(fact[:], disc[:], ACT.Exp, scale=-1.0).then_inc(s_fact, 1)
            for c in range(DC):
                act.wait_ge(s_x[c], 16)
                copy(x_hi[:, c, :], xT_raw[:, c, :]).then_inc(s_xh, 1)
                if c == 0:
                    split_raw(0)
            act.wait_ge(s_fact, 1)
            for m in range(G + 1):
                split_raw(JOB["fuse", m])
                act.wait_ge(s_t, m + 1)
                if m >= 2:
                    wait_stage2(act, m - 2)
                scale = {} if m == 0 else {"scale": fact[:, m - 1:m]}
                copy(l_hi[:, m % 2, :], term_tile[m], **scale).then_inc(s_lhi, 1)
                step_functions(("term", m))
            split_raw(JOB["in", 0])
            for i in range(2 * C1):
                if i % 2 == 0 and i // 2 + 1 < C1:
                    split_raw(JOB["in", i // 2 + 1])
                step_functions(("pair", 1, i))
                silu(i, 1)
            for f in range(C1):
                split_raw(JOB["out", f])
                split_h(("out", f))
                step_functions(("down", 1, f))
            step_functions(("norm", 1))
            act.wait_ge(s_ln, 1)
            nc.scalar.activation(std[:, 1, :], std[:, 0, :], ACT.Sqrt).then_inc(s_sqrt, 1)

            def split_nf4(f):
                j, m = JOB["nf4in", f], rows(f, F2)
                act.wait_ge(s_tr, f + 1)
                wait_w_slot(act, j)
                copy(w_hi[:, j % 2, 0:2 * DC * m].rearrange("p (c m) -> p c m", m=m),
                     PS[:, 6:8, :].rearrange("p b (c m) -> p (b c) m", m=P)[:, :, 0:m]).then_inc(s_whi, 1)

            split_nf4(0)
            for t in range(TT):
                act.wait_ge(s_xtr, t + 1)
                copy(x_hi[:, :, t * P:(t + 1) * P],
                     PS[:, t % 6, :].rearrange("p (c t) -> p c t", c=DC)).then_inc(s_xh, 1)
            for i in range(2 * C2):
                step_functions(("pair", 2, i))
                silu(i, 2)
                if i % 2 == 0 and i // 2 + 1 < C2:
                    split_nf4(i // 2 + 1)
            act.wait_ge(s_wlo, RAW_JOBS)
            for q in range(2):
                step_functions(("w3", q))
                for c in range(C2):
                    m, n = rows(c, F2), q * C2 + c
                    act.wait_ge(s_w3tr, n + 1)
                    dst = w3T[0:m, c * D + q * 2 * P:c * D + (q + 1) * 2 * P].rearrange("p (j r) -> p r j", r=2)
                    copy(dst, PS[0:m, 6 + n % 2, 0:2 * P].rearrange("p (r j) -> p r j", r=2)).then_inc(s_w3T, 1)
            for c in range(C2):
                j, p = JOB["nf4out", c], rows(c, F2)
                if c == 0:
                    act.wait_ge(s_w3T, 2 * C2)
                wait_w_slot(act, j)
                copy(w_hi[0:p, j % 2, 0:D], w3T[0:p, c * D:(c + 1) * D]).then_inc(s_whi, 1)
                split_h(("nf4out", c))
            for b in range(2):
                act.wait_ge(s_ln, 2 + b)
                nc.scalar.activation(std[:, 1, 4 * b:4 * b + 4], std[:, 0, 4 * b:4 * b + 4],
                                     ACT.Sqrt).then_inc(s_sqrt, 1)

        @block.vector
        def _(dve):
            v = nc.vector
            small = [0]

            def link(ins):
                small[0] += 1
                ins.then_inc(s_st, 1)
                dve.wait_ge(s_st, small[0])

            def scales(u):
                slot, p, width = unit_shape(u)
                n = width // BLOCK
                if u < C2:
                    dve.wait_ge(s_q[u], 32)
                else:
                    dve.wait_ge(s_q[3 * W3_UNITS[u - C2][0]], 48)
                v.tensor_reduce(amax[0:p, u, 0:n], quant_view(u).rearrange("p (b e) -> p b e", e=BLOCK), AX_X,
                                ALU.max, apply_absolute_value=True).then_inc(s_prep, 1)
                dve.wait_ge(s_prep, 3 * u + 1)
                v.tensor_scalar(rcp[0:p, u, 0:n], amax[0:p, u, 0:n], TINY, None, ALU.max).then_inc(s_prep, 1)
                dve.wait_ge(s_prep, 3 * u + 2)
                v.reciprocal(rcp[0:p, u, 0:n], rcp[0:p, u, 0:n]).then_inc(s_prep, 1)

            def add_steps(key):
                a, b = PLAN[key]
                for s in range(a, b):
                    for u in PREPS[s]:
                        scales(u)
                    u, k = STEPS[s]
                    _, p, width = unit_shape(u)
                    sum_, step = acc[0:p, u % 2, 0:width], relu[0:p, s % NR, 0:width]
                    dve.wait_ge(s_relu, s + 1)
                    if k == 0:
                        if u >= 2:
                            dve.wait_ge(s_dq, u - 1)
                        v.tensor_scalar(sum_, step, RISE[0], float(CODE[0]), ALU.min, ALU.add).then_inc(s_step, 1)
                    else:
                        dve.wait_ge(s_step, STEPS.index((u, k - 1)) + 1)
                        v.scalar_tensor_tensor(sum_, step, RISE[k], sum_, ALU.min, ALU.add).then_inc(s_step, 1)

            def gate_times_up(i, layer):
                f, half, g = i // 2, i % 2, i + (layer - 1) * 2 * C1
                p, bank = rows(f, F1 if layer == 1 else F2), 2 * ((i + 1) % 3)
                hv = h[0:p, f * TOK + half * HALF:f * TOK + (half + 1) * HALF]
                dve.wait_ge(s_silu, g + 1)
                v.tensor_tensor(hv, PS[0:p, bank + 1, :], hv, ALU.mult).then_inc(s_h, 1)

            def add_tiles(n0, tiles):
                for t in tiles:
                    dve.wait_ge(s_tile, n0 + t + 1)
                    v.tensor_tensor(R[:, t, :], PS[:, t, :], R[:, t, :], ALU.add).then_inc(s_y, 1)

            def layernorm(n0, y0, sq, tiles):
                a, b = tiles[0], tiles[-1] + 1
                for t in tiles:
                    dve.wait_ge(s_y, y0 + t + 1)
                    ins = v.bn_stats(stats[:, t, :], R[:, t, :])
                    small[0] += 1
                    ins.then_inc(s_st, 1)
                for t in tiles:
                    dve.wait_ge(s_st, small[0])
                    ins = v.bn_aggr(mv[:, t, :], stats[:, t, :])
                    ins.then_inc(s_st, 1)
                small[0] += len(tiles)
                dve.wait_ge(s_st, small[0])
                var, root, inv, tmp, tmp2 = (std[:, r, a:b] for r in range(5))
                v.tensor_scalar(var, mv[:, a:b, 1], EPS, None, ALU.add).then_inc(s_ln, 1)
                dve.wait_ge(s_sqrt, sq)
                link(v.reciprocal(inv, root))
                link(v.tensor_tensor(tmp, inv, inv, ALU.mult))
                link(v.tensor_tensor(tmp2, tmp, var, ALU.mult))
                link(v.tensor_scalar(tmp, tmp2, -0.5, 1.5, ALU.mult, ALU.add))
                link(v.tensor_tensor(tmp2, inv, tmp, ALU.mult))
                for t in tiles:
                    v.tensor_scalar(R[:, t, :], R[:, t, :], mv[:, t, 0:1], std[:, 4, t:t + 1], ALU.subtract,
                                    ALU.mult).then_inc(s_norm, 1)

            for c in range(DC):
                dve.wait_ge(s_xh, c + 1)
                v.tensor_tensor(x_lo[:, c, :], xT_raw[:, c, :], x_hi[:, c, :].bitcast(F32),
                                ALU.subtract).then_inc(s_xl, 1)
            dve.wait_ge(s_point, 32)
            dve.wait_ge(s_pre, 1)
            v.tensor_copy(up, PS[:, 0:2, :].rearrange("p b n -> p (b n)")).then_inc(s_t, 1)
            v.tensor_scalar(delta, PS[:, 2:4, :].rearrange("p b n -> p (b n)"), point_sb[:, 0:1], None,
                            ALU.subtract).then_inc(s_pre_read, 1)
            dve.wait_ge(s_pre_read, 1)
            v.scalar_tensor_tensor(kept, delta, THD, delta, ALU.is_le, ALU.mult).then_inc(s_keep, 1)
            dve.wait_ge(s_keep, 1)
            v.scalar_tensor_tensor(kept, delta, -THD, kept, ALU.is_ge, ALU.mult).then_inc(s_keep, 1)
            for m in range(G + 1):
                if m < G:
                    dve.wait_ge(s_t, m + 1)
                    if m >= 2:
                        dve.wait_ge(s_lhi, m)
                    if m + 1 == KEEP_FROM:
                        dve.wait_ge(s_keep, 2)
                    v.tensor_tensor(term_tile[m + 1], term_tile[m], kept if m + 1 == KEEP_FROM else delta,
                                    ALU.mult).then_inc(s_t, 1)
                dve.wait_ge(s_lhi, m + 1)
                if m == 1:
                    dve.wait_ge(s_fact, 1)
                if m >= 2:
                    wait_stage2(dve, m - 2)
                scale = 1.0 if m == 0 else fact[:, m - 1:m]
                v.scalar_tensor_tensor(l_lo[:, m % 2, :], term_tile[m], scale, l_hi[:, m % 2, :].bitcast(F32),
                                       ALU.mult, ALU.subtract).then_inc(s_llo_t, 1)
                add_steps(("term", m))
            dve.wait_ge(s_R, 16)
            add_tiles(0, range(TT))
            for i in range(2 * C1):
                add_steps(("pair", 1, i))
                gate_times_up(i, 1)
            for f in range(C1):
                add_steps(("down", 1, f))
            add_steps(("norm", 1))
            dve.wait_ge(s_y, TT)
            add_tiles(TT, range(TT))
            layernorm(0, TT, 1, range(TT))

            def lo_nf4(f):
                j, m = JOB["nf4in", f], rows(f, F2)
                dve.wait_ge(s_whi, j + 1)
                wait_w_slot(dve, j)
                n = 2 * DC * m
                v.tensor_tensor(w_lo[:, j % 2, 0:n].rearrange("p (c m) -> p c m", m=m),
                                PS[:, 6:8, :].rearrange("p b (c m) -> p (b c) m", m=P)[:, :, 0:m],
                                w_hi[:, j % 2, 0:n].bitcast(F32).rearrange("p (c m) -> p c m", m=m),
                                ALU.subtract).then_inc(s_wlo4, 1)

            lo_nf4(0)
            for t in range(TT):
                dve.wait_ge(s_xh, DC + t + 1)
                v.tensor_tensor(x_lo[:, :, t * P:(t + 1) * P],
                                PS[:, t % 6, :].rearrange("p (c t) -> p c t", c=DC),
                                x_hi[:, :, t * P:(t + 1) * P].bitcast(F32), ALU.subtract).then_inc(s_xl, 1)
            for i in range(2 * C2):
                add_steps(("pair", 2, i))
                gate_times_up(i, 2)
                if i % 2 == 0 and i // 2 + 1 < C2:
                    lo_nf4(i // 2 + 1)
            for q in range(2):
                add_steps(("w3", q))
            for b in range(2):
                tiles = range(4 * b, 4 * b + 4)
                add_tiles(2 * TT, tiles)
                layernorm(TT, 2 * TT, 2 + b, tiles)

        @block.gpsimd
        def _(pool):
            g = nc.gpsimd

            def scale_units(key):
                a, b = PLAN[key]
                for s in range(a, b):
                    for u in PREPS[s]:
                        _, p, width = unit_shape(u)
                        pool.wait_ge(s_prep, 3 * u + 3)
                        q = quant_view(u).rearrange("p (b e) -> p b e", e=BLOCK)
                        g.tensor_tensor(q, q, scale_view(rcp, u), ALU.mult).then_inc(s_nrm, 1)
                    u, k = STEPS[s]
                    if k == NB - 1:
                        _, p, width = unit_shape(u)
                        pool.wait_ge(s_step, s + 1)
                        g.tensor_tensor(quant_view(u).rearrange("p (b e) -> p b e", e=BLOCK),
                                        acc[0:p, u % 2, 0:width].rearrange("p (b e) -> p b e", e=BLOCK),
                                        scale_view(amax, u), ALU.mult).then_inc(s_dq, 1)

            def lo_raw(j):
                p, n = job_shape(j)
                pool.wait_ge(s_whi, j + 1)
                wait_w_slot(pool, j)
                g.tensor_tensor(w_lo[0:p, j % 2, 0:n], w_raw(j)[0:p, 0:n], w_hi[0:p, j % 2, 0:n].bitcast(F32),
                                ALU.subtract).then_inc(s_wlo, 1)

            def lo_h(job):
                kind, f = job
                p, n = rows(f, F1 if kind == "out" else F2), LHS[job]
                pool.wait_ge(s_lhi, n + 1)
                wait_stage2(pool, n - 2)
                g.tensor_tensor(l_lo[0:p, n % 2, :], h[0:p, f * TOK:(f + 1) * TOK],
                                l_hi[0:p, n % 2, :].bitcast(F32), ALU.subtract).then_inc(s_llo_h, 1)

            lo_raw(0)
            for m in range(G + 1):
                lo_raw(JOB["fuse", m])
                scale_units(("term", m))
            lo_raw(JOB["in", 0])
            for i in range(2 * C1):
                if i % 2 == 0 and i // 2 + 1 < C1:
                    lo_raw(JOB["in", i // 2 + 1])
                scale_units(("pair", 1, i))
            for f in range(C1):
                lo_raw(JOB["out", f])
                lo_h(("out", f))
                scale_units(("down", 1, f))
            scale_units(("norm", 1))
            for i in range(2 * C2):
                scale_units(("pair", 2, i))
            for q in range(2):
                scale_units(("w3", q))
            for c in range(C2):
                j, p = JOB["nf4out", c], rows(c, F2)
                pool.wait_ge(s_whi, j + 1)
                wait_w_slot(pool, j)
                g.tensor_tensor(w_lo[0:p, j % 2, 0:D], w3T[0:p, c * D:(c + 1) * D],
                                w_hi[0:p, j % 2, 0:D].bitcast(F32), ALU.subtract).then_inc(s_wlo, 1)
                lo_h(("nf4out", c))

        @block.tensor
        def _(pe):
            t_ = nc.tensor

            def product(dst, a_hi, a_lo, b_hi, b_lo, start, stop):
                t_.matmul(dst, a_hi, b_hi, start=start, stop=False)
                t_.matmul(dst, a_hi, b_lo, start=False, stop=False)
                return t_.matmul(dst, a_lo, b_hi, start=False, stop=stop)

            def wait_job(j):
                pe.wait_ge(s_whi, j + 1)
                if JOBS[j][0] == "nf4in":
                    pe.wait_ge(s_wlo4, JOBS[j][1] + 1)
                else:
                    pe.wait_ge(s_wlo, lo_jobs_raw(j))

            def project(j, kind, half, bank, m):
                wh = w_hi[:, j % 2, 0:2 * DC * m].rearrange("p (g c m) -> p g c m", g=2, c=DC)
                wl = w_lo[:, j % 2, 0:2 * DC * m].rearrange("p (g c m) -> p g c m", g=2, c=DC)
                for c in range(DC):
                    xs = slice(half * HALF, (half + 1) * HALF)
                    last = product(PS[0:m, bank, :], wh[:, kind, c, :], wl[:, kind, c, :], x_hi[:, c, xs],
                                   x_lo[:, c, xs], c == 0, c == DC - 1)
                return last

            def pair(i, layer, job):
                f, half, m = i // 2, i % 2, rows(i // 2, F1 if layer == 1 else F2)
                bank = 2 * ((i + 1) % 3)
                if half == 0:
                    wait_job(job)
                if i >= 3:
                    pe.wait_ge(s_h, i - 2 + (layer - 1) * 2 * C1)
                elif layer == 1:
                    pe.wait_ge(s_y, bank + 2)
                else:
                    pe.wait_ge(s_xl, DC + (4 if i == 0 else TT))
                project(job, 0, half, bank, m)
                last = project(job, 1, half, bank + 1, m)
                last.then_inc(s_pair, 1)

            def stage2(job, first, last_chunk):
                kind, f = job
                j, n = JOB[job], LHS[job]
                p = P if kind == "fuse" else rows(f, F1 if kind == "out" else F2)
                wait_job(j)
                pe.wait_ge(s_lhi, n + 1)
                if kind == "fuse":
                    pe.wait_ge(s_llo_t, n + 1)
                else:
                    pe.wait_ge(s_llo_h, n - G)
                for t in range(TT):
                    ts = slice(t * P, (t + 1) * P)
                    last = product(PS[:, t, :], l_hi[0:p, n % 2, ts], l_lo[0:p, n % 2, ts], w_hi[0:p, j % 2, 0:D],
                                   w_lo[0:p, j % 2, 0:D], first, last_chunk)
                    if last_chunk:
                        last.then_inc(s_tile, 1)
                    elif t == TT - 1:
                        last.then_inc(s_l_used, 1)

            def transpose_nf4(f):
                m = rows(f, F2)
                pe.wait_ge(s_dq, f + 1)
                if f >= 1:
                    pe.wait_ge(s_wlo4, f)
                for g_ in range(2):
                    for c in range(DC):
                        last = t_.transpose(PS[:, 6 + g_, c * P:c * P + m],
                                            Q[0:m, f, g_ * D + c * P:g_ * D + (c + 1) * P], ident[0:m, 0:m])
                last.then_inc(s_tr, 1)

            wait_job(0)
            wh0 = w_hi[:, 0, :].rearrange("p (g c m) -> p g c m", g=2, c=DC)
            wl0 = w_lo[:, 0, :].rearrange("p (g c m) -> p g c m", g=2, c=DC)
            for c in range(DC):
                pe.wait_ge(s_xh, c + 1)
                pe.wait_ge(s_xl, c + 1)
                for kind in range(2):
                    for half in range(2):
                        xs = slice(half * HALF, (half + 1) * HALF)
                        last = product(PS[:, 2 * kind + half, :], wh0[:, kind, c, :], wl0[:, kind, c, :],
                                       x_hi[:, c, xs], x_lo[:, c, xs], c == 0, c == DC - 1)
            last.then_inc(s_pre, 1)
            pe.wait_ge(s_pre_read, 1)
            for m in range(G + 1):
                stage2(("fuse", m), m == 0, m == G)
            for i in range(2 * C1):
                pair(i, 1, JOB["in", i // 2])
            pe.wait_ge(s_h, 2 * C1)
            for f in range(C1):
                stage2(("out", f), f == 0, f == C1 - 1)
            pe.wait_ge(s_ident, 16)
            pe.wait_ge(s_y, 2 * TT)
            transpose_nf4(0)
            for t in range(TT):
                pe.wait_ge(s_norm, t + 1)
                if t >= 6:
                    pe.wait_ge(s_xl, DC + t - 5)
                for c in range(DC):
                    last = t_.transpose(PS[:, t % 6, c * P:(c + 1) * P], R[:, t, c * P:(c + 1) * P], ident[:])
                last.then_inc(s_xtr, 1)
            for i in range(2 * C2):
                pair(i, 2, JOB["nf4in", i // 2])
                if i % 2 == 0 and i // 2 + 1 < C2:
                    transpose_nf4(i // 2 + 1)
            for q in range(2):
                pe.wait_ge(s_dq, C2 + 3 * (q + 1))
                tile = Q[:, 3 * q:3 * q + 3, :].rearrange("p a n -> p (a n)")
                for c in range(C2):
                    m, n = rows(c, F2), q * C2 + c
                    if n >= 2:
                        pe.wait_ge(s_w3T, n - 1)
                    else:
                        pe.wait_ge(s_wlo4, C2)
                    for r in range(2):
                        last = t_.transpose(PS[0:m, 6 + n % 2, r * P:(r + 1) * P],
                                            tile[:, r * F2 + c * P:r * F2 + c * P + m], ident[:])
                    last.then_inc(s_w3tr, 1)
            pe.wait_ge(s_h, 2 * C1 + 2 * C2)
            pe.wait_ge(s_w3T, 2 * C2)
            for c in range(C2):
                stage2(("nf4out", c), c == 0, c == C2 - 1)


def kernel(L0_attn_hidden_states, L0_attn_up_w, L0_attn_gate_w, L0_attn_local_point, L0_attn_local_approx_output,
           L0_attn_fuse_weight, L0_attn_discount_factor, L0_attn_ffn_gate_w, L0_attn_ffn_up_w, L0_attn_ffn_down_w,
           L0_ffn_w1, L0_ffn_w2, L0_ffn_w3):
    import concourse.bacc as bacc
    from concourse.bass_utils import run_bass_kernel_spmd

    def a(t):
        return np.asarray(t)

    def chunks_in(*ws):
        width = ws[0].shape[0]
        parts = []
        for f in range(-(-width // P)):
            m = min(P, width - f * P)
            both = np.stack([w[f * P:f * P + m].reshape(m, DC, P) for w in ws])
            parts.append(both.transpose(3, 0, 2, 1).reshape(P, 2 * DC * m))
        return np.ascontiguousarray(np.concatenate(parts, axis=1))

    x = a(L0_attn_hidden_states)
    x2 = x.reshape(TOK, D)
    fuse = a(L0_attn_fuse_weight)
    arrays = {
        "xT": np.ascontiguousarray(x2.T.reshape(DC, P, TOK).transpose(1, 0, 2)),
        "xN": np.ascontiguousarray(x2.reshape(TT, P, D).transpose(1, 0, 2)),
        "w_pre": chunks_in(a(L0_attn_up_w), a(L0_attn_gate_w)),
        "w_fuse": np.ascontiguousarray(np.stack([a(L0_attn_local_approx_output).T]
                                                + [fuse[:, :, g].T for g in range(G)])),
        "w_in": chunks_in(a(L0_attn_ffn_gate_w), a(L0_attn_ffn_up_w)),
        "w_out": np.ascontiguousarray(a(L0_attn_ffn_down_w).T),
        "point": a(L0_attn_local_point).reshape(S, 1),
        "discount": a(L0_attn_discount_factor).reshape(1, G),
        "w1": np.ascontiguousarray(a(L0_ffn_w1)),
        "w2": np.ascontiguousarray(a(L0_ffn_w2)),
        "w3": np.ascontiguousarray(a(L0_ffn_w3)).reshape(D // 2, PAIR),
        "ident_in": np.eye(P, dtype=np.float32),
    }
    nc = bacc.Bacc("TRN2", target_bir_lowering=False, num_devices=1)
    args = {name: nc.dram_tensor(name, v.shape, mybir.dt.from_np(v.dtype), kind="ExternalInput").ap()
            for name, v in arrays.items()}
    out = nc.dram_tensor("out", (TOK, D), F32, kind="ExternalOutput").ap()
    build(nc, **args, out=out)
    r = run_bass_kernel_spmd(nc, [arrays], core_ids=[0])
    return r.results[0]["out"].reshape(x.shape)
```

```python
from contextlib import ExitStack

import numpy as np
import concourse.bass as bass
from concourse import mybir

F32 = mybir.dt.float32
F32R = mybir.dt.float32r
BF16 = mybir.dt.bfloat16
ALU = mybir.AluOpType
ACT = mybir.ActivationFunctionType
AX_X = mybir.AxisListType.X

P = 128
TOK = 1024
D = 512
DC = D // P
HALF = 512
TT = TOK // P
S = 128
G = 6
F1 = 1248
F2 = 1376
C1 = -(-F1 // P)
C2 = -(-F2 // P)
KEEP_FROM = 5
THD = 2.5
EPS = 1e-5
BLOCK = 64
TINY = 1.1754943508222875e-38

CODE = np.array([-1.0, -0.6961928009986877, -0.5250730514526367, -0.39491748809814453, -0.28444138169288635,
                 -0.18477343022823334, -0.09105003625154495, 0.0, 0.07958029955625534, 0.16093020141124725,
                 0.24611230194568634, 0.33791524171829224, 0.44070982933044434, 0.5626170039176941,
                 0.7229568362236023, 1.0], dtype=np.float32)
BOUND = (CODE[:-1] + CODE[1:]) * np.float32(0.5)
NB = len(BOUND)
STEEP = 2.0 ** 60


def code_rises():
    rises = []
    for k in range(NB):
        r = np.float32(CODE[k + 1] - CODE[k])
        near = (r, np.nextafter(r, np.float32(2)), np.nextafter(r, np.float32(0)))
        rises.append(float([x for x in near if np.float32(CODE[k] + x) == CODE[k + 1]][0]))
    return rises


RISE = code_rises()

UW = 1024
PAIR = 2 * F2
PAIR_BLOCKS = PAIR // BLOCK
ROW_BLOCKS = PAIR_BLOCKS // 2
W3_PARTS = 3
NARROW = ROW_BLOCKS // W3_PARTS
UNITS = C2 + 2 * W3_PARTS


def unit_rows(u):
    return min(P, F2 - u * P) if u < C2 else P


def unit_width(u):
    return UW if u < C2 or (u - C2) % W3_PARTS == 2 else 2 * NARROW * BLOCK


def w3_unit_of(q, c):
    return C2 + W3_PARTS * q + min(2, (2 * c + 2) // NARROW)


W3_LATER = 8
STEPS = [(u, k) for _, u, k in sorted((NB * u + 1.8 * k + (W3_LATER if u >= C2 else 0), u, k)
                                      for u in range(UNITS) for k in range(NB))]
FIRST = {u: STEPS.index((u, 0)) for u in range(UNITS)}
LAST = {u: STEPS.index((u, NB - 1)) for u in range(UNITS)}
LEAD = 6
PREP = {u: max(0, FIRST[u] - LEAD) for u in range(UNITS)}
PREPS = {s: [u for u in range(UNITS) if PREP[u] == s] for s in range(len(STEPS))}

START_STEPS, TERM_STEPS, PAIR_STEPS, DOWN_STEPS, NORM_STEPS, FFN_STEPS, LAST_STEPS = 4, 3, 4.25, 4, 2, 4, 2.3
AHEAD = 2


def deal():
    done, plan, most = 0, {}, PREP[C2]

    def give(key, upto):
        nonlocal done
        upto = min(most, max(done, int(upto)))
        plan[key] = (done, upto)
        done = upto

    give("start", START_STEPS)
    for m in range(G + 1):
        give(("term", m), done + TERM_STEPS)
    base = done
    for i in range(2 * C1):
        give(("pair", 1, i), base + PAIR_STEPS * (i + 1))
    base = done
    for f in range(C1):
        give(("down", 1, f), base + DOWN_STEPS * (f + 1))
    give("norm", max(done + NORM_STEPS, LAST[0] + 1))
    base = done
    for i in range(2 * C2):
        need = LAST[min(i // 2 + 1, C2 - 1)] + 1 if i % 2 == 0 else 0
        most = PREP[C2] if i < 3 else PREP[C2 + W3_PARTS] if i < 9 else len(STEPS)
        give(("pair", 2, i), max(base + FFN_STEPS * (i + 1), need))
    give("w3", LAST[w3_unit_of(0, AHEAD - 1)] + 1)
    base = done
    for n in range(2 * C2):
        ahead = min(n + AHEAD, 2 * C2 - 1)
        give(("down", 2, n), max(base + LAST_STEPS * (n + 1), LAST[w3_unit_of(ahead // C2, ahead % C2)] + 1))
    assert done == len(STEPS)
    return plan


PLAN = deal()

JOBS = ([("pre", 0)] + [("fuse", m) for m in range(G + 1)] + [("in", f) for f in range(C1)]
        + [("out", f) for f in range(C1)] + [("nf4in", f) for f in range(C2)]
        + [("nf4out", n) for n in range(2 * C2)])
JOB = {job: j for j, job in enumerate(JOBS)}
RAW_JOBS = 1 + (G + 1) + 2 * C1
RAW_SLOTS = 5
LHS = {("fuse", m): m for m in range(G + 1)}
LHS.update({("out", f): G + 1 + f for f in range(C1)})
LHS.update({("nf4out", n): G + 1 + C1 + n for n in range(2 * C2)})
LASTS = [G, G + C1, G + C1 + C2, G + C1 + 2 * C2]
ADD_FIRST = C2
VECTOR_LO = [("out", f) for f in range(C1)] + [("nf4out", n) for n in range(C2 + 6, 2 * C2)]
GPSIMD_LO = [job for job in LHS if job[0] != "fuse" and job not in VECTOR_LO]


def rows(f, width):
    return min(P, width - f * P)


def job_rows(job):
    kind, f = job
    return P if kind == "fuse" else rows(f, F1) if kind == "out" else rows(f % C2, F2)


def build(nc, xT, xN, w_pre, w_fuse, w_in, w_out, point, discount, w1, w2, w3, ident_in, out):
    with ExitStack() as ctx:
        def sb(name, shape, dt=F32):
            return ctx.enter_context(nc.sbuf_tensor(name, shape, dt))

        def sem(name):
            return ctx.enter_context(nc.semaphore(name))

        x_hi, x_lo = sb("x_hi", [P, DC, TOK], F32R), sb("x_lo", [P, DC, TOK], F32R)
        R = sb("R", [P, TT, D])
        h = sb("h", [P, C2 * TOK])
        w_hi, w_lo = sb("w_hi", [P, 2, 1024], F32R), sb("w_lo", [P, 2, 1024], F32R)
        l_hi, l_lo = sb("l_hi", [P, 2, TOK], F32R), sb("l_lo", [P, 2, TOK], F32R)
        w3T = sb("w3T", [P, C2 * D])
        Q = sb("Q", [P, C2, UW])
        acc = sb("acc", [P, 2, UW])
        NR = 3
        relu = sb("relu", [P, NR, UW], BF16)
        amax, rcp = sb("amax", [P, UNITS, UW // BLOCK]), sb("rcp", [P, UNITS, UW // BLOCK])
        ident = sb("ident", [P, P])
        point_sb, disc, fact = sb("point_sb", [P, 1]), sb("disc", [P, G]), sb("fact", [P, G])
        stats, mv = sb("stats", [P, TT, 6]), sb("mv", [P, TT, 2])
        std = sb("std", [P, 5, TT])
        PS = ctx.enter_context(nc.psum_tensor("PS", [P, 8, 512], F32))

        xT_raw = h[:, 0:DC * TOK].rearrange("p (c t) -> p c t", c=DC)
        up, delta, ta, tb, kept = (h[:, (DC + i) * TOK:(DC + i + 1) * TOK] for i in range(5))
        term_tile = [up, ta, tb, ta, tb, ta, tb]

        def w_raw(j):
            return w3T[:, (j % RAW_SLOTS) * 1024:(j % RAW_SLOTS) * 1024 + 1024]

        def job_shape(j):
            kind, f = JOBS[j]
            if kind in ("pre",):
                return P, 2 * DC * P
            if kind == "fuse":
                return P, D
            if kind == "in":
                return P, 2 * DC * rows(f, F1)
            return rows(f, F1), D

        s_point = sem("s_point")
        s_ident = sem("s_ident")
        s_x = [sem(f"s_x{c}") for c in range(DC)]
        s_R = sem("s_R")
        s_raw = [sem(f"s_raw{i}") for i in range(RAW_SLOTS)]
        s_q = [sem(f"s_q{i}") for i in range(C2)]
        s_out = sem("s_out")
        s_fact = sem("s_fact")
        s_xh, s_xl = sem("s_xh"), sem("s_xl")
        s_whi = sem("s_whi")
        s_wlo = sem("s_wlo")
        s_wlo4 = sem("s_wlo4")
        s_lhi = sem("s_lhi")
        s_llo_t = sem("s_llo_t")
        s_llo_h = sem("s_llo_h")
        s_llo_v = sem("s_llo_v")
        s_pre = sem("s_pre")
        s_pre_read = sem("s_pre_read")
        s_t = sem("s_t")
        s_keep = sem("s_keep")
        s_pair = sem("s_pair")
        s_silu = sem("s_silu")
        s_h = sem("s_h")
        s_l_used = sem("s_l_used")
        s_tile = sem("s_tile")
        s_y = sem("s_y")
        s_st, s_ln, s_sqrt, s_norm = sem("s_st"), sem("s_ln"), sem("s_sqrt"), sem("s_norm")
        s_xtr = sem("s_xtr")
        s_prep = sem("s_prep")
        s_nrm = sem("s_nrm")
        s_relu = sem("s_relu")
        s_step = sem("s_step")
        s_dq = sem("s_dq")
        s_tr = sem("s_tr")
        s_w3tr = sem("s_w3tr")
        s_w3T = sem("s_w3T")

        block = ctx.enter_context(nc.Block())

        def wait_stage2(eng, n):
            if n in LASTS:
                eng.wait_ge(s_tile, TT * (LASTS.index(n) + 1))
            else:
                eng.wait_ge(s_l_used, n + 1 - sum(1 for x in LASTS if x < n))

        def wait_w_slot(eng, j):
            if j < 2:
                return
            kind, f = JOBS[j - 2]
            if kind == "pre":
                eng.wait_ge(s_pre, 1)
            elif kind in ("in", "nf4in"):
                eng.wait_ge(s_pair, 2 * (f + 1) + (2 * C1 if kind == "nf4in" else 0))
            else:
                wait_stage2(eng, LHS[JOBS[j - 2]])

        def lo_jobs_raw(j):
            return sum(1 for kind, _ in JOBS[:j + 1] if kind != "nf4in")

        def unit_count(u):
            return sum(2 if x >= C2 and (x - C2) % W3_PARTS == 2 else 1 for x in range(u + 1))

        def scaled(u):
            return 3 * unit_count(u)

        normalised = quantised = unit_count

        def w3_tile(q):
            return Q[:, W3_PARTS * q:W3_PARTS * (q + 1), :].rearrange("p a n -> p (a n)")

        def unit_read(u):
            if u < C2:
                return Q[0:unit_rows(u), u, :]
            q, a = divmod(u - C2, W3_PARTS)
            row = ROW_BLOCKS * BLOCK
            if a < 2:
                return w3_tile(q)[:, 0:2 * row].rearrange("p (r n) -> p r n", r=2)[
                    :, :, a * NARROW * BLOCK:(a + 1) * NARROW * BLOCK]
            return w3_tile(q)[:, BLOCK:BLOCK + 2 * row].rearrange("p (r n) -> p r n", r=2)[
                :, :, (2 * NARROW - 1) * BLOCK:]

        def unit_parts(u):
            p = unit_rows(u)
            if u < C2:
                return [(Q[0:p, u, :].rearrange("p (b e) -> p b e", e=BLOCK), 0, UW // BLOCK)]
            q, a = divmod(u - C2, W3_PARTS)
            if a < 2:
                return [(unit_read(u).rearrange("p r (b e) -> p r b e", e=BLOCK), 0, 2 * NARROW)]
            first = w3_tile(q)[:, 2 * NARROW * BLOCK:3 * NARROW * BLOCK]
            second = w3_tile(q)[:, PAIR - (NARROW + 1) * BLOCK:PAIR]
            return [(first.rearrange("p (b e) -> p b e", e=BLOCK), 0, NARROW),
                    (second.rearrange("p (b e) -> p b e", e=BLOCK), NARROW + 1, NARROW + 1)]

        def per_block(t, u, b, n):
            v = t[0:unit_rows(u), u, b:b + n]
            return v.rearrange("p (r b) -> p r b", r=2) if n == 2 * NARROW else v

        def spread(t, u, b, n):
            v, p = per_block(t, u, b, n), unit_rows(u)
            if n == 2 * NARROW:
                return v.unsqueeze(3).broadcast_to([p, 2, NARROW, BLOCK])
            return v.unsqueeze(2).broadcast_to([p, n, BLOCK])

        def out_bank(q, t):
            return t // 2 if q == 0 else (4, 5, 0, 1)[t // 2]

        @block.sync
        def _(sp):
            def load_job(j):
                kind, f = JOBS[j]
                if j >= RAW_SLOTS:
                    sp.wait_ge(s_wlo, j - RAW_SLOTS + 1)
                p, n = job_shape(j)
                src = {"pre": lambda: w_pre, "fuse": lambda: w_fuse[f], "in": lambda: w_in[:, f * 1024:f * 1024 + n],
                       "out": lambda: w_out[f * P:f * P + p, :]}[kind]()
                sp.dma_start(w_raw(j)[0:p, 0:n], src).then_inc(s_raw[j % RAW_SLOTS], 16)

            def load_unit(u):
                p = unit_rows(u)
                sp.dma_start(Q[0:p, u, 0:D], w1[u * P:u * P + p, :]).then_inc(s_q[u], 16)
                sp.dma_start(Q[0:p, u, D:2 * D], w2[u * P:u * P + p, :]).then_inc(s_q[u], 16)

            load_job(0)
            for c in range(DC):
                sp.dma_start(xT_raw[:, c, :], xT[:, c, :]).then_inc(s_x[c], 16)
            sp.dma_start(point_sb[:], point).then_inc(s_point, 16)
            sp.dma_start(disc[:], discount.broadcast_to([P, G])).then_inc(s_point, 16)
            load_unit(0)
            load_job(1)
            load_unit(1)
            for j in range(2, RAW_SLOTS):
                load_job(j)
            sp.dma_start(R[:], xN).then_inc(s_R, 16)
            sp.dma_start(ident[:], ident_in).then_inc(s_ident, 16)
            for u in range(2, C2):
                load_unit(u)
            for j in range(RAW_SLOTS, RAW_JOBS):
                load_job(j)
            for q in range(2):
                sp.wait_ge(s_tr, 3 * q + 3)
                sp.dma_start(w3_tile(q)[:, 0:PAIR], w3[q * P:(q + 1) * P, :]).then_inc(s_q[3 * q], 16)
            for t in range(TT):
                sp.wait_ge(s_norm, TT + t + 1)
                sp.dma_start(out[t * P:(t + 1) * P, :], R[:, t, :]).then_inc(s_out, 16)
            sp.wait_ge(s_out, 16 * TT)

        @block.scalar
        def _(act):
            def copy(dst, src, **kw):
                return nc.scalar.activation(dst, src, ACT.Copy, **kw)

            def step_functions(key):
                a, b = PLAN[key]
                for s in range(a, b):
                    u, k = STEPS[s]
                    p, width = unit_rows(u), unit_width(u)
                    if k == 0:
                        act.wait_ge(s_nrm, normalised(u))
                        if u >= C2 and (u - C2) % W3_PARTS == 2:
                            act.wait_ge(s_dq, quantised(u - 2))
                    if s >= NR:
                        act.wait_ge(s_step, s - NR + 1)
                    dst = relu[0:p, s % NR, 0:width]
                    if u >= C2:
                        dst = dst.rearrange("p (r n) -> p r n", r=2)
                    nc.scalar.activation(dst, unit_read(u), ACT.Relu, scale=STEEP,
                                         bias=float(-BOUND[k]) * STEEP).then_inc(s_relu, 1)

            def split_raw(j):
                p, n = job_shape(j)
                act.wait_ge(s_raw[j % RAW_SLOTS], 16 * (j // RAW_SLOTS + 1))
                wait_w_slot(act, j)
                copy(w_hi[0:p, j % 2, 0:n], w_raw(j)[0:p, 0:n]).then_inc(s_whi, 1)

            def split_h(job):
                kind, f = job
                f, p, n = f % C2, job_rows(job), LHS[job]
                act.wait_ge(s_h, 2 * (f + 1) + (2 * C1 if kind == "nf4out" else 0))
                wait_stage2(act, n - 2)
                copy(l_hi[0:p, n % 2, :], h[0:p, f * TOK:(f + 1) * TOK]).then_inc(s_lhi, 1)

            def silu(i, layer):
                f, half, g = i // 2, i % 2, i + (layer - 1) * 2 * C1
                p, bank = rows(f, F1 if layer == 1 else F2), 2 * ((i + 1) % 3)
                act.wait_ge(s_pair, g + 1)
                if layer == 2 and i == 0:
                    act.wait_ge(s_llo_v, C1)
                nc.scalar.activation(h[0:p, f * TOK + half * HALF:f * TOK + (half + 1) * HALF], PS[0:p, bank, :],
                                     ACT.Silu).then_inc(s_silu, 1)

            for c in range(DC):
                act.wait_ge(s_x[c], 16)
                copy(x_hi[:, c, :], xT_raw[:, c, :]).then_inc(s_xh, 1)
                if c == 0:
                    split_raw(0)
            act.wait_ge(s_point, 32)
            nc.scalar.activation(fact[:], disc[:], ACT.Exp, scale=-1.0).then_inc(s_fact, 1)
            step_functions("start")
            act.wait_ge(s_fact, 1)
            for m in range(G + 1):
                split_raw(JOB["fuse", m])
                act.wait_ge(s_t, m + 1)
                if m >= 2:
                    wait_stage2(act, m - 2)
                scale = {} if m == 0 else {"scale": fact[:, m - 1:m]}
                copy(l_hi[:, m % 2, :], term_tile[m], **scale).then_inc(s_lhi, 1)
                step_functions(("term", m))
            split_raw(JOB["in", 0])
            for i in range(2 * C1):
                if i % 2 == 0 and i // 2 + 1 < C1:
                    split_raw(JOB["in", i // 2 + 1])
                step_functions(("pair", 1, i))
                silu(i, 1)
            for f in range(C1):
                split_raw(JOB["out", f])
                split_h(("out", f))
                step_functions(("down", 1, f))
            act.wait_ge(s_ln, 1)
            nc.scalar.activation(std[:, 1, :], std[:, 0, :], ACT.Sqrt).then_inc(s_sqrt, 1)
            step_functions("norm")

            def split_nf4(f):
                j, m = JOB["nf4in", f], rows(f, F2)
                act.wait_ge(s_tr, f + 1)
                wait_w_slot(act, j)
                copy(w_hi[:, j % 2, 0:2 * DC * m].rearrange("p (c m) -> p c m", m=m),
                     PS[:, 6:8, :].rearrange("p b (c m) -> p (b c) m", m=P)[:, :, 0:m]).then_inc(s_whi, 1)

            split_nf4(0)
            for t in range(TT):
                act.wait_ge(s_xtr, t + 1)
                copy(x_hi[:, :, t * P:(t + 1) * P],
                     PS[:, t % 6, :].rearrange("p (c t) -> p c t", c=DC)).then_inc(s_xh, 1)
            for i in range(2 * C2):
                step_functions(("pair", 2, i))
                silu(i, 2)
                if i % 2 == 0 and i // 2 + 1 < C2:
                    split_nf4(i // 2 + 1)
            act.wait_ge(s_wlo, RAW_JOBS)
            step_functions("w3")

            def fetch_w3(n):
                q, c = divmod(n, C2)
                m = rows(c, F2)
                act.wait_ge(s_w3tr, n + 1)
                dst = w3T[0:m, c * D + q * 2 * P:c * D + (q + 1) * 2 * P].rearrange("p (j r) -> p r j", r=2)
                copy(dst, PS[0:m, 6 + n % 2, 0:2 * P].rearrange("p (r j) -> p r j", r=2)).then_inc(s_w3T, 1)

            for n in range(AHEAD):
                fetch_w3(n)
            for n in range(2 * C2):
                j, p, (q, c) = JOB["nf4out", n], job_rows(("nf4out", n)), divmod(n, C2)
                step_functions(("down", 2, n))
                if n + AHEAD < 2 * C2:
                    fetch_w3(n + AHEAD)
                act.wait_ge(s_w3T, n + 1)
                wait_w_slot(act, j)
                copy(w_hi[0:p, j % 2, 0:2 * P],
                     w3T[0:p, c * D + q * 2 * P:c * D + (q + 1) * 2 * P]).then_inc(s_whi, 1)
                split_h(("nf4out", n))
            for b in range(2):
                act.wait_ge(s_ln, 2 + b)
                nc.scalar.activation(std[:, 1, 4 * b:4 * b + 4], std[:, 0, 4 * b:4 * b + 4],
                                     ACT.Sqrt).then_inc(s_sqrt, 1)

        @block.vector
        def _(dve):
            v = nc.vector
            small = [0]

            def link(ins):
                small[0] += 1
                ins.then_inc(s_st, 1)
                dve.wait_ge(s_st, small[0])

            def scales(u):
                p, done = unit_rows(u), scaled(u - 1)
                dve.wait_ge(s_q[u if u < C2 else W3_PARTS * ((u - C2) // W3_PARTS)], 32 if u < C2 else 48)
                parts = unit_parts(u)
                for blocks, b, n in parts:
                    v.tensor_reduce(per_block(amax, u, b, n), blocks, AX_X, ALU.max,
                                    apply_absolute_value=True).then_inc(s_prep, 1)
                for i, (_, b, n) in enumerate(parts):
                    dve.wait_ge(s_prep, done + i + 1)
                    v.tensor_scalar(rcp[0:p, u, b:b + n], amax[0:p, u, b:b + n], TINY, None,
                                    ALU.max).then_inc(s_prep, 1)
                for i, (_, b, n) in enumerate(parts):
                    dve.wait_ge(s_prep, done + len(parts) + i + 1)
                    v.reciprocal(rcp[0:p, u, b:b + n], rcp[0:p, u, b:b + n]).then_inc(s_prep, 1)

            def add_steps(key):
                a, b = PLAN[key]
                for s in range(a, b):
                    for u in PREPS[s]:
                        scales(u)
                    u, k = STEPS[s]
                    p, width = unit_rows(u), unit_width(u)
                    sum_, step = acc[0:p, u % 2, 0:width], relu[0:p, s % NR, 0:width]
                    dve.wait_ge(s_relu, s + 1)
                    if k == 0:
                        if u >= 2:
                            dve.wait_ge(s_dq, quantised(u - 2))
                        v.tensor_scalar(sum_, step, RISE[0], float(CODE[0]), ALU.min, ALU.add).then_inc(s_step, 1)
                    else:
                        dve.wait_ge(s_step, STEPS.index((u, k - 1)) + 1)
                        v.scalar_tensor_tensor(sum_, step, RISE[k], sum_, ALU.min, ALU.add).then_inc(s_step, 1)

            def gate_times_up(i, layer):
                f, half, g = i // 2, i % 2, i + (layer - 1) * 2 * C1
                p, bank = rows(f, F1 if layer == 1 else F2), 2 * ((i + 1) % 3)
                hv = h[0:p, f * TOK + half * HALF:f * TOK + (half + 1) * HALF]
                dve.wait_ge(s_silu, g + 1)
                v.tensor_tensor(hv, PS[0:p, bank + 1, :], hv, ALU.mult).then_inc(s_h, 1)

            def add_tiles(n0, tiles):
                for t in tiles:
                    dve.wait_ge(s_tile, n0 + t + 1)
                    v.tensor_tensor(R[:, t, :], PS[:, t, :], R[:, t, :], ALU.add).then_inc(s_y, 1)

            def layernorm(n0, added, sq, tiles):
                a, b = tiles[0], tiles[-1] + 1
                for t in tiles:
                    dve.wait_ge(s_y, added[t])
                    ins = v.bn_stats(stats[:, t, :], R[:, t, :])
                    small[0] += 1
                    ins.then_inc(s_st, 1)
                for t in tiles:
                    dve.wait_ge(s_st, small[0])
                    ins = v.bn_aggr(mv[:, t, :], stats[:, t, :])
                    ins.then_inc(s_st, 1)
                small[0] += len(tiles)
                dve.wait_ge(s_st, small[0])
                var, root, inv, tmp, tmp2 = (std[:, r, a:b] for r in range(5))
                v.tensor_scalar(var, mv[:, a:b, 1], EPS, None, ALU.add).then_inc(s_ln, 1)
                dve.wait_ge(s_sqrt, sq)
                link(v.reciprocal(inv, root))
                link(v.tensor_tensor(tmp, inv, inv, ALU.mult))
                link(v.tensor_tensor(tmp2, tmp, var, ALU.mult))
                link(v.tensor_scalar(tmp, tmp2, -0.5, 1.5, ALU.mult, ALU.add))
                link(v.tensor_tensor(tmp2, inv, tmp, ALU.mult))
                for t in tiles:
                    v.tensor_scalar(R[:, t, :], R[:, t, :], mv[:, t, 0:1], std[:, 4, t:t + 1], ALU.subtract,
                                    ALU.mult).then_inc(s_norm, 1)

            for c in range(DC):
                dve.wait_ge(s_xh, c + 1)
                v.tensor_tensor(x_lo[:, c, :], xT_raw[:, c, :], x_hi[:, c, :].bitcast(F32),
                                ALU.subtract).then_inc(s_xl, 1)
            add_steps("start")
            dve.wait_ge(s_point, 32)
            dve.wait_ge(s_pre, 1)
            v.tensor_copy(up, PS[:, 0:2, :].rearrange("p b n -> p (b n)")).then_inc(s_t, 1)
            v.tensor_scalar(delta, PS[:, 2:4, :].rearrange("p b n -> p (b n)"), point_sb[:, 0:1], None,
                            ALU.subtract).then_inc(s_pre_read, 1)
            dve.wait_ge(s_pre_read, 1)
            v.scalar_tensor_tensor(kept, delta, THD, delta, ALU.is_le, ALU.mult).then_inc(s_keep, 1)
            dve.wait_ge(s_keep, 1)
            v.scalar_tensor_tensor(kept, delta, -THD, kept, ALU.is_ge, ALU.mult).then_inc(s_keep, 1)
            for m in range(G + 1):
                if m < G:
                    dve.wait_ge(s_t, m + 1)
                    if m >= 2:
                        dve.wait_ge(s_lhi, m)
                    if m + 1 == KEEP_FROM:
                        dve.wait_ge(s_keep, 2)
                    v.tensor_tensor(term_tile[m + 1], term_tile[m], kept if m + 1 == KEEP_FROM else delta,
                                    ALU.mult).then_inc(s_t, 1)
                dve.wait_ge(s_lhi, m + 1)
                if m == 1:
                    dve.wait_ge(s_fact, 1)
                if m >= 2:
                    wait_stage2(dve, m - 2)
                scale = 1.0 if m == 0 else fact[:, m - 1:m]
                v.scalar_tensor_tensor(l_lo[:, m % 2, :], term_tile[m], scale, l_hi[:, m % 2, :].bitcast(F32),
                                       ALU.mult, ALU.subtract).then_inc(s_llo_t, 1)
                add_steps(("term", m))
            dve.wait_ge(s_R, 16)
            add_tiles(0, range(TT))
            for i in range(2 * C1):
                add_steps(("pair", 1, i))
                gate_times_up(i, 1)
            def lo_h(job):
                c, l, p = job[1] % C2, LHS[job], job_rows(job)
                dve.wait_ge(s_lhi, l + 1)
                wait_stage2(dve, l - 2)
                v.tensor_tensor(l_lo[0:p, l % 2, :], h[0:p, c * TOK:(c + 1) * TOK],
                                l_hi[0:p, l % 2, :].bitcast(F32), ALU.subtract).then_inc(s_llo_v, 1)

            for f in range(C1):
                if ("out", f) in VECTOR_LO:
                    lo_h(("out", f))
                add_steps(("down", 1, f))
            dve.wait_ge(s_y, TT)
            add_tiles(TT, range(TT))
            layernorm(0, [TT + t + 1 for t in range(TT)], 1, range(TT))
            add_steps("norm")

            def lo_nf4(f):
                j, m = JOB["nf4in", f], rows(f, F2)
                dve.wait_ge(s_whi, j + 1)
                wait_w_slot(dve, j)
                n = 2 * DC * m
                v.tensor_tensor(w_lo[:, j % 2, 0:n].rearrange("p (c m) -> p c m", m=m),
                                PS[:, 6:8, :].rearrange("p b (c m) -> p (b c) m", m=P)[:, :, 0:m],
                                w_hi[:, j % 2, 0:n].bitcast(F32).rearrange("p (c m) -> p c m", m=m),
                                ALU.subtract).then_inc(s_wlo4, 1)

            lo_nf4(0)
            for t in range(TT):
                dve.wait_ge(s_xh, DC + t + 1)
                v.tensor_tensor(x_lo[:, :, t * P:(t + 1) * P],
                                PS[:, t % 6, :].rearrange("p (c t) -> p c t", c=DC),
                                x_hi[:, :, t * P:(t + 1) * P].bitcast(F32), ALU.subtract).then_inc(s_xl, 1)
            for i in range(2 * C2):
                add_steps(("pair", 2, i))
                gate_times_up(i, 2)
                if i % 2 == 0 and i // 2 + 1 < C2:
                    lo_nf4(i // 2 + 1)
            add_steps("w3")

            def add_columns(q, b):
                cols = slice(q * 2 * P, (q + 1) * 2 * P)
                dve.wait_ge(s_tile, TT * (2 + q) + 2 * b + 2)
                rv = R[:, 2 * b:2 * b + 2, cols]
                v.tensor_tensor(rv, PS[:, out_bank(q, 2 * b), :].rearrange("p (t n) -> p t n", t=2), rv,
                                ALU.add).then_inc(s_y, 1)

            for n in range(2 * C2):
                add_steps(("down", 2, n))
                if n == ADD_FIRST:
                    for b in range(TT // 2):
                        add_columns(0, b)
                if ("nf4out", n) in VECTOR_LO:
                    lo_h(("nf4out", n))
            for b in range(2):
                for i in range(2):
                    add_columns(1, 2 * b + i)
                layernorm(TT, [2 * TT + TT // 2 + t // 2 + 1 for t in range(TT)], 2 + b, range(4 * b, 4 * b + 4))

        @block.gpsimd
        def _(pool):
            g = nc.gpsimd

            def scale_units(key):
                a, b = PLAN[key]
                for s in range(a, b):
                    for u in PREPS[s]:
                        pool.wait_ge(s_prep, scaled(u))
                        for blocks, b0, n in unit_parts(u):
                            g.tensor_tensor(blocks, blocks, spread(rcp, u, b0, n), ALU.mult).then_inc(s_nrm, 1)
                    u, k = STEPS[s]
                    if k == NB - 1:
                        pool.wait_ge(s_step, s + 1)
                        for blocks, b0, n in unit_parts(u):
                            codes = acc[0:unit_rows(u), u % 2, b0 * BLOCK:(b0 + n) * BLOCK]
                            codes = (codes.rearrange("p (r b e) -> p r b e", r=2, e=BLOCK) if n == 2 * NARROW
                                     else codes.rearrange("p (b e) -> p b e", e=BLOCK))
                            g.tensor_tensor(blocks, codes, spread(amax, u, b0, n), ALU.mult).then_inc(s_dq, 1)

            def lo_raw(j):
                p, n = job_shape(j)
                pool.wait_ge(s_whi, j + 1)
                wait_w_slot(pool, j)
                g.tensor_tensor(w_lo[0:p, j % 2, 0:n], w_raw(j)[0:p, 0:n], w_hi[0:p, j % 2, 0:n].bitcast(F32),
                                ALU.subtract).then_inc(s_wlo, 1)

            def lo_h(job):
                f, p, n = job[1] % C2, job_rows(job), LHS[job]
                pool.wait_ge(s_lhi, n + 1)
                wait_stage2(pool, n - 2)
                g.tensor_tensor(l_lo[0:p, n % 2, :], h[0:p, f * TOK:(f + 1) * TOK],
                                l_hi[0:p, n % 2, :].bitcast(F32), ALU.subtract).then_inc(s_llo_h, 1)

            lo_raw(0)
            scale_units("start")
            for m in range(G + 1):
                lo_raw(JOB["fuse", m])
                scale_units(("term", m))
            lo_raw(JOB["in", 0])
            for i in range(2 * C1):
                if i % 2 == 0 and i // 2 + 1 < C1:
                    lo_raw(JOB["in", i // 2 + 1])
                scale_units(("pair", 1, i))
            for f in range(C1):
                lo_raw(JOB["out", f])
                if ("out", f) in GPSIMD_LO:
                    lo_h(("out", f))
                scale_units(("down", 1, f))
            scale_units("norm")
            for i in range(2 * C2):
                scale_units(("pair", 2, i))
            scale_units("w3")
            for n in range(2 * C2):
                j, p, (q, c) = JOB["nf4out", n], job_rows(("nf4out", n)), divmod(n, C2)
                scale_units(("down", 2, n))
                pool.wait_ge(s_whi, j + 1)
                wait_w_slot(pool, j)
                g.tensor_tensor(w_lo[0:p, j % 2, 0:2 * P], w3T[0:p, c * D + q * 2 * P:c * D + (q + 1) * 2 * P],
                                w_hi[0:p, j % 2, 0:2 * P].bitcast(F32), ALU.subtract).then_inc(s_wlo, 1)
                if ("nf4out", n) in GPSIMD_LO:
                    lo_h(("nf4out", n))

        @block.tensor
        def _(pe):
            t_ = nc.tensor

            def product(dst, a_hi, a_lo, b_hi, b_lo, start, stop, shared=False):
                t_.matmul(dst, a_hi, b_hi, start=start, stop=False, skip_group_check=shared)
                t_.matmul(dst, a_hi, b_lo, start=False, stop=False, skip_group_check=shared)
                return t_.matmul(dst, a_lo, b_hi, start=False, stop=stop, skip_group_check=shared)

            def wait_job(j):
                pe.wait_ge(s_whi, j + 1)
                if JOBS[j][0] == "nf4in":
                    pe.wait_ge(s_wlo4, JOBS[j][1] + 1)
                else:
                    pe.wait_ge(s_wlo, lo_jobs_raw(j))

            def project(j, kind, half, bank, m):
                wh = w_hi[:, j % 2, 0:2 * DC * m].rearrange("p (g c m) -> p g c m", g=2, c=DC)
                wl = w_lo[:, j % 2, 0:2 * DC * m].rearrange("p (g c m) -> p g c m", g=2, c=DC)
                for c in range(DC):
                    xs = slice(half * HALF, (half + 1) * HALF)
                    last = product(PS[0:m, bank, :], wh[:, kind, c, :], wl[:, kind, c, :], x_hi[:, c, xs],
                                   x_lo[:, c, xs], c == 0, c == DC - 1)
                return last

            def pair(i, layer, job):
                f, half, m = i // 2, i % 2, rows(i // 2, F1 if layer == 1 else F2)
                bank = 2 * ((i + 1) % 3)
                if half == 0:
                    wait_job(job)
                if i >= 3:
                    pe.wait_ge(s_h, i - 2 + (layer - 1) * 2 * C1)
                elif layer == 1:
                    pe.wait_ge(s_y, bank + 2)
                else:
                    pe.wait_ge(s_xl, DC + (4 if i == 0 else TT))
                project(job, 0, half, bank, m)
                last = project(job, 1, half, bank + 1, m)
                last.then_inc(s_pair, 1)

            def stage2(job, first, last_chunk):
                kind, f = job
                j, n, p = JOB[job], LHS[job], job_rows(job)
                width = 2 * P if kind == "nf4out" else D
                wait_job(j)
                pe.wait_ge(s_lhi, n + 1)
                if kind == "fuse":
                    pe.wait_ge(s_llo_t, n + 1)
                elif job in VECTOR_LO:
                    pe.wait_ge(s_llo_v, VECTOR_LO.index(job) + 1)
                else:
                    pe.wait_ge(s_llo_h, GPSIMD_LO.index(job) + 1)
                for t in range(TT):
                    ts = slice(t * P, (t + 1) * P)
                    dst, start = PS[:, t, :], first
                    if kind == "nf4out":
                        if first and f >= C2 and t >= 4 and t % 2 == 0:
                            pe.wait_ge(s_y, 2 * TT + t // 2 - 1)
                        dst = PS[:, out_bank(f // C2, t), (t % 2) * width:(t % 2 + 1) * width]
                        start = first and t % 2 == 0
                    last = product(dst, l_hi[0:p, n % 2, ts], l_lo[0:p, n % 2, ts], w_hi[0:p, j % 2, 0:width],
                                   w_lo[0:p, j % 2, 0:width], start, last_chunk, kind == "nf4out")
                    if last_chunk:
                        last.then_inc(s_tile, 1)
                    elif t == TT - 1:
                        last.then_inc(s_l_used, 1)

            def transpose_nf4(f):
                m = rows(f, F2)
                pe.wait_ge(s_dq, quantised(f))
                if f >= 1:
                    pe.wait_ge(s_wlo4, f)
                for g_ in range(2):
                    for c in range(DC):
                        last = t_.transpose(PS[:, 6 + g_, c * P:c * P + m],
                                            Q[0:m, f, g_ * D + c * P:g_ * D + (c + 1) * P], ident[0:m, 0:m])
                last.then_inc(s_tr, 1)

            wait_job(0)
            wh0 = w_hi[:, 0, :].rearrange("p (g c m) -> p g c m", g=2, c=DC)
            wl0 = w_lo[:, 0, :].rearrange("p (g c m) -> p g c m", g=2, c=DC)
            for c in range(DC):
                pe.wait_ge(s_xh, c + 1)
                pe.wait_ge(s_xl, c + 1)
                for kind in range(2):
                    for half in range(2):
                        xs = slice(half * HALF, (half + 1) * HALF)
                        last = product(PS[:, 2 * kind + half, :], wh0[:, kind, c, :], wl0[:, kind, c, :],
                                       x_hi[:, c, xs], x_lo[:, c, xs], c == 0, c == DC - 1)
            last.then_inc(s_pre, 1)
            pe.wait_ge(s_pre_read, 1)
            for m in range(G + 1):
                stage2(("fuse", m), m == 0, m == G)
            for i in range(2 * C1):
                pair(i, 1, JOB["in", i // 2])
            pe.wait_ge(s_h, 2 * C1)
            for f in range(C1):
                stage2(("out", f), f == 0, f == C1 - 1)
            pe.wait_ge(s_ident, 16)
            pe.wait_ge(s_y, 2 * TT)
            transpose_nf4(0)
            for t in range(TT):
                pe.wait_ge(s_norm, t + 1)
                if t >= 6:
                    pe.wait_ge(s_xl, DC + t - 5)
                for c in range(DC):
                    last = t_.transpose(PS[:, t % 6, c * P:(c + 1) * P], R[:, t, c * P:(c + 1) * P], ident[:])
                last.then_inc(s_xtr, 1)
            for i in range(2 * C2):
                pair(i, 2, JOB["nf4in", i // 2])
                if i % 2 == 0 and i // 2 + 1 < C2:
                    transpose_nf4(i // 2 + 1)

            def transpose_w3(n):
                q, c = divmod(n, C2)
                m = rows(c, F2)
                pe.wait_ge(s_dq, quantised(w3_unit_of(q, c)))
                if n >= 2:
                    pe.wait_ge(s_w3T, n - 1)
                else:
                    pe.wait_ge(s_wlo4, C2)
                for r in range(2):
                    last = t_.transpose(PS[0:m, 6 + n % 2, r * P:(r + 1) * P],
                                        w3_tile(q)[:, r * F2 + c * P:r * F2 + c * P + m], ident[:])
                last.then_inc(s_w3tr, 1)

            for n in range(AHEAD + 1):
                transpose_w3(n)
            pe.wait_ge(s_h, 2 * C1 + 2 * C2)
            for n in range(2 * C2):
                if n + AHEAD + 1 < 2 * C2:
                    transpose_w3(n + AHEAD + 1)
                stage2(("nf4out", n), n % C2 == 0, n % C2 == C2 - 1)


def kernel(L0_attn_hidden_states, L0_attn_up_w, L0_attn_gate_w, L0_attn_local_point, L0_attn_local_approx_output,
           L0_attn_fuse_weight, L0_attn_discount_factor, L0_attn_ffn_gate_w, L0_attn_ffn_up_w, L0_attn_ffn_down_w,
           L0_ffn_w1, L0_ffn_w2, L0_ffn_w3):
    import concourse.bacc as bacc
    from concourse.bass_utils import run_bass_kernel_spmd

    def a(t):
        return np.asarray(t)

    def chunks_in(*ws):
        width = ws[0].shape[0]
        parts = []
        for f in range(-(-width // P)):
            m = min(P, width - f * P)
            both = np.stack([w[f * P:f * P + m].reshape(m, DC, P) for w in ws])
            parts.append(both.transpose(3, 0, 2, 1).reshape(P, 2 * DC * m))
        return np.ascontiguousarray(np.concatenate(parts, axis=1))

    x = a(L0_attn_hidden_states)
    x2 = x.reshape(TOK, D)
    fuse = a(L0_attn_fuse_weight)
    arrays = {
        "xT": np.ascontiguousarray(x2.T.reshape(DC, P, TOK).transpose(1, 0, 2)),
        "xN": np.ascontiguousarray(x2.reshape(TT, P, D).transpose(1, 0, 2)),
        "w_pre": chunks_in(a(L0_attn_up_w), a(L0_attn_gate_w)),
        "w_fuse": np.ascontiguousarray(np.stack([a(L0_attn_local_approx_output).T]
                                                + [fuse[:, :, g].T for g in range(G)])),
        "w_in": chunks_in(a(L0_attn_ffn_gate_w), a(L0_attn_ffn_up_w)),
        "w_out": np.ascontiguousarray(a(L0_attn_ffn_down_w).T),
        "point": a(L0_attn_local_point).reshape(S, 1),
        "discount": a(L0_attn_discount_factor).reshape(1, G),
        "w1": np.ascontiguousarray(a(L0_ffn_w1)),
        "w2": np.ascontiguousarray(a(L0_ffn_w2)),
        "w3": np.ascontiguousarray(a(L0_ffn_w3)).reshape(D // 2, PAIR),
        "ident_in": np.eye(P, dtype=np.float32),
    }
    nc = bacc.Bacc("TRN2", target_bir_lowering=False, num_devices=1)
    args = {name: nc.dram_tensor(name, v.shape, mybir.dt.from_np(v.dtype), kind="ExternalInput").ap()
            for name, v in arrays.items()}
    out = nc.dram_tensor("out", (TOK, D), F32, kind="ExternalOutput").ap()
    build(nc, **args, out=out)
    r = run_bass_kernel_spmd(nc, [arrays], core_ids=[0])
    return r.results[0]["out"].reshape(x.shape)
```

```python
from contextlib import ExitStack

import numpy as np
import concourse.bass as bass
from concourse import mybir

F32 = mybir.dt.float32
F32R = mybir.dt.float32r
BF16 = mybir.dt.bfloat16
ALU = mybir.AluOpType
ACT = mybir.ActivationFunctionType
AX_X = mybir.AxisListType.X

P = 128
TOK = 1024
D = 512
DC = D // P
HALF = 512
TT = TOK // P
S = 128
G = 6
F1 = 1248
F2 = 1376
C1 = -(-F1 // P)
C2 = -(-F2 // P)
KEEP_FROM = 5
THD = 2.5
EPS = 1e-5
NR = 4
BLOCK = 64
TINY = 1.1754943508222875e-38

CODE = np.array([-1.0, -0.6961928009986877, -0.5250730514526367, -0.39491748809814453, -0.28444138169288635,
                 -0.18477343022823334, -0.09105003625154495, 0.0, 0.07958029955625534, 0.16093020141124725,
                 0.24611230194568634, 0.33791524171829224, 0.44070982933044434, 0.5626170039176941,
                 0.7229568362236023, 1.0], dtype=np.float32)
BOUND = (CODE[:-1] + CODE[1:]) * np.float32(0.5)
NB = len(BOUND)
STEEP = 2.0 ** 60


def code_rises():
    rises = []
    for k in range(NB):
        r = np.float32(CODE[k + 1] - CODE[k])
        near = (r, np.nextafter(r, np.float32(2)), np.nextafter(r, np.float32(0)))
        rises.append(float([x for x in near if np.float32(CODE[k] + x) == CODE[k + 1]][0]))
    return rises


RISE = code_rises()

UW = 1024
PAIR = 2 * F2
PAIR_BLOCKS = PAIR // BLOCK
ROW_BLOCKS = PAIR_BLOCKS // 2
W3_PARTS = 3
NARROW = ROW_BLOCKS // W3_PARTS
UNITS = C2 + 2 * W3_PARTS


def unit_rows(u):
    return min(P, F2 - u * P) if u < C2 else P


def unit_width(u):
    return UW if u < C2 or (u - C2) % W3_PARTS == 2 else 2 * NARROW * BLOCK


def w3_unit_of(q, c):
    return C2 + W3_PARTS * q + min(2, (2 * c + 2) // NARROW)


STEPS = [(u, k) for _, u, k in sorted((NB * u + 1.8 * k, u, k)
                                      for u in range(UNITS) for k in range(NB))]
FIRST = {u: STEPS.index((u, 0)) for u in range(UNITS)}
LAST = {u: STEPS.index((u, NB - 1)) for u in range(UNITS)}
LEAD = 7
PREP = {u: max(0, FIRST[u] - LEAD) for u in range(UNITS)}
PREPS = {s: [u for u in range(UNITS) if PREP[u] == s] for s in range(len(STEPS))}

START_STEPS, TERM_STEPS, PAIR_STEPS, DOWN_STEPS, TILE_STEPS, FFN_STEPS, LAST_STEPS = 2, 3, 3.9, 3.5, 2.5, 4, 2.1
TILE_UNTIL = 6
AHEAD = 2
H_SLOTS = 6
H_AHEAD = 4
EARLY = 2
TAIL = 3
NORM_GROUPS = [range(0, 4), range(4, 8)]


def deal():
    done, plan, most = 0, {}, PREP[C2]

    def give(key, upto):
        nonlocal done
        upto = min(most, max(done, int(upto)))
        plan[key] = (done, upto)
        done = upto

    give("start", START_STEPS)
    for m in range(G + 1):
        give(("term", m), START_STEPS + TERM_STEPS * m)
    base = done
    for i in range(2 * C1):
        give(("pair", 1, i), base + PAIR_STEPS * (i + 1))
    base = done
    for f in range(C1 - TAIL):
        give(("down", 1, f), base + DOWN_STEPS * (f + 1))
    base = done
    for t in range(TT):
        give(("tile", t), max(base + TILE_STEPS * min(t + 1, TILE_UNTIL), LAST[0] + 1 if t == 0 else 0))
    base, most = done, len(STEPS)
    for i in range(2 * C2):
        need = LAST[min(i // 2 + 1, C2 - 1)] + 1 if i % 2 == 0 else 0
        if i == 2 * C2 - 2:
            need = LAST[w3_unit_of(0, AHEAD - 1)] + 1
        give(("pair", 2, i), max(base + FFN_STEPS * (i + 1), need))
    base = done
    for n in range(2 * C2):
        ahead = min(n + AHEAD, 2 * C2 - 1)
        give(("down", 2, n), max(base + LAST_STEPS * (n + 1), LAST[w3_unit_of(ahead // C2, ahead % C2)] + 1))
    assert done == len(STEPS)
    return plan


PLAN = deal()

JOBS = ([("pre", 0)] + [("fuse", m) for m in range(G + 1)] + [("in", f) for f in range(C1)]
        + [("out", f) for f in range(C1)] + [("nf4in", f) for f in range(C2)]
        + [("nf4out", n) for n in range(2 * C2)])
JOB = {job: j for j, job in enumerate(JOBS)}
RAW_JOBS = 1 + (G + 1) + 2 * C1
RAW_SLOTS = 5
H_JOBS = [("out", f) for f in range(C1)] + [("nf4out", n) for n in range(2 * C2)]
VECTOR_LO = [("out", f) for f in range(H_AHEAD, C1, 2)]
GPSIMD_LO = [job for job in H_JOBS if job not in VECTOR_LO]
STAGE2 = {job: n for n, job in enumerate([("fuse", m) for m in range(G + 1)] + [("out", f) for f in range(C1)]
                                         + [("nf4out", n) for n in range(2 * C2)])}
SUMS = [(G + 1, 1), (C1, TAIL), (C2, 1), (C2, TAIL)]
ENDS = [stop for n0, (count, tail) in zip([0, G + 1, G + 1 + C1, G + 1 + C1 + C2], SUMS)
        for stop in [(n0 + count - tail, n0 + count)]]


def rows(f, width):
    return min(P, width - f * P)


def job_rows(job):
    kind, f = job
    return P if kind == "fuse" else rows(f, F1) if kind == "out" else rows(f % C2, F2)


def build(nc, xT, xN, w_pre, w_fuse, w_in, w_out, point, discount, w1, w2, w3, ident_in, out):
    with ExitStack() as ctx:
        def sb(name, shape, dt=F32):
            return ctx.enter_context(nc.sbuf_tensor(name, shape, dt))

        def sem(name):
            return ctx.enter_context(nc.semaphore(name))

        x_hi, x_lo = sb("x_hi", [P, DC, TOK], F32R), sb("x_lo", [P, DC, TOK], F32R)
        R = sb("R", [P, TT, D])
        h = sb("h", [P, C2 * TOK])
        w_hi, w_lo = sb("w_hi", [P, 2, 1024], F32R), sb("w_lo", [P, 2, 1024], F32R)
        l_hi, l_lo = sb("l_hi", [P, 2, TOK], F32R), sb("l_lo", [P, 2, TOK], F32R)
        raw = sb("raw", [P, 2 * PAIR])
        Q = sb("Q", [P, C2, UW])
        acc = sb("acc", [P, 2, UW])
        relu = sb("relu", [P, NR, UW], BF16)
        amax, rcp = sb("amax", [P, 4, UW // BLOCK]), sb("rcp", [P, 2, UW // BLOCK])
        ident = sb("ident", [P, P])
        point_sb, disc, fact = sb("point_sb", [P, 1]), sb("disc", [P, G]), sb("fact", [P, G])
        stats, mv = sb("stats", [P, TT, 2, 6]), sb("mv", [P, TT, 2])
        std = sb("std", [P, 5, TT])
        PS = ctx.enter_context(nc.psum_tensor("PS", [P, 8, 512], F32))

        xT_raw = h[:, 0:DC * TOK].rearrange("p (c t) -> p c t", c=DC)
        delta, ta, tb, kept = (h[:, (DC + i) * TOK:(DC + i + 1) * TOK] for i in range(4))
        term_tile = [None, ta, tb, ta, tb, ta, tb]

        def w_raw(j):
            return raw[:, (j % RAW_SLOTS) * 1024:(j % RAW_SLOTS) * 1024 + 1024]

        def narrow(j):
            return {"fuse": 2, "out": 2, "nf4out": 4}.get(JOBS[j][0], 1)

        def w_slot(w, j, p, n):
            first = (j // 2) % narrow(j) * (1024 // narrow(j))
            return w[0:p, j % 2, first:first + n]

        h_slots = ([(l_hi[:, i, :], l_lo[:, i, :]) for i in range(2)]
                   + [(x[:, 2 * i, :], x[:, 2 * i + 1, :]) for x in (x_lo, x_hi) for i in range(2)])
        assert len(h_slots) == H_SLOTS

        def job_shape(j):
            kind, f = JOBS[j]
            if kind in ("pre",):
                return P, 2 * DC * P
            if kind == "fuse":
                return P, D
            if kind == "in":
                return P, 2 * DC * rows(f, F1)
            return rows(f, F1), D

        s_point = sem("s_point")
        s_ident = sem("s_ident")
        s_x = [sem(f"s_x{c}") for c in range(DC)]
        s_R = sem("s_R")
        s_raw = [sem(f"s_raw{i}") for i in range(RAW_SLOTS)]
        s_q = [sem(f"s_q{i}") for i in range(C2)]
        s_w3 = [sem(f"s_w3_{q}") for q in range(2)]
        s_out = sem("s_out")
        s_fact = sem("s_fact")
        s_xh, s_xl = sem("s_xh"), sem("s_xl")
        s_whi = sem("s_whi")
        s_wlo0 = sem("s_wlo0")
        s_wlo = sem("s_wlo")
        s_wlo4 = sem("s_wlo4")
        s_lhi = sem("s_lhi")
        s_llo_t = sem("s_llo_t")
        s_llo_h = sem("s_llo_h")
        s_llo_v = sem("s_llo_v")
        s_pre = sem("s_pre")
        s_pre_read = sem("s_pre_read")
        s_t = sem("s_t")
        s_keep = sem("s_keep")
        s_pair = sem("s_pair")
        s_silu = sem("s_silu")
        s_h = sem("s_h")
        s_l_used = sem("s_l_used")
        s_tile = sem("s_tile")
        s_y = sem("s_y")
        s_st, s_ln, s_sqrt, s_norm = sem("s_st"), sem("s_ln"), sem("s_sqrt"), sem("s_norm")
        s_xtr = sem("s_xtr")
        s_prep = sem("s_prep")
        s_nrm = sem("s_nrm")
        s_relu = sem("s_relu")
        s_step = sem("s_step")
        s_dq = sem("s_dq")
        s_tr = sem("s_tr")
        s_w3tr = sem("s_w3tr")

        block = ctx.enter_context(nc.Block())

        def wait_stage2(eng, n):
            for i, (first, stop) in enumerate(ENDS):
                if first <= n < stop:
                    eng.wait_ge(s_tile, TT * (i + 1))
                    return
            eng.wait_ge(s_l_used, n + 1 - sum(stop - first for first, stop in ENDS if stop <= n))

        def wait_w_slot(eng, j):
            kind, f = JOBS[j]
            before = j - 2 * narrow(j) if f >= 2 * narrow(j) or narrow(j) == 1 else JOB[kind, f % 2] - 2
            if before < 0:
                return
            kind, f = JOBS[before]
            if kind == "pre":
                eng.wait_ge(s_pre, 2)
            elif kind in ("in", "nf4in"):
                eng.wait_ge(s_pair, 2 * (f + 1) + (2 * C1 if kind == "nf4in" else 0))
            else:
                wait_stage2(eng, STAGE2[JOBS[before]])

        def wait_h_slot(eng, job):
            kind, c = job
            layer = 1 if kind == "out" else 2
            if c >= H_SLOTS:
                wait_stage2(eng, STAGE2[kind, c - H_SLOTS])
            elif c < EARLY:
                eng.wait_ge(s_tile, TT * layer)
            else:
                eng.wait_ge(s_pair, 2 * C1 + (2 * C2 if layer == 2 else 0))

        def pair_bank(layer, i):
            return 2 * ((i + layer - 1) % 3)

        def lo_of_h(eng, ops, job, done):
            p, c = job_rows(job), job[1] % C2
            hi, lo = h_slots[job[1] % H_SLOTS]
            eng.wait_ge(s_lhi, G + 1 + H_JOBS.index(job) + 1)
            wait_h_slot(eng, job)
            ops.tensor_tensor(lo[0:p, :], h[0:p, c * TOK:(c + 1) * TOK], hi[0:p, :].bitcast(F32),
                              ALU.subtract).then_inc(done, 1)

        def unit_count(u):
            return sum(2 if x >= C2 and (x - C2) % W3_PARTS == 2 else 1 for x in range(u + 1))

        def scaled(u):
            return 3 * unit_count(u)

        normalised = quantised = unit_count

        def w3_tile(q):
            return raw[:, q * PAIR:(q + 1) * PAIR]

        def unit_read(u):
            if u < C2:
                return Q[0:unit_rows(u), u, :]
            q, a = divmod(u - C2, W3_PARTS)
            row = ROW_BLOCKS * BLOCK
            if a < 2:
                return w3_tile(q)[:, 0:2 * row].rearrange("p (r n) -> p r n", r=2)[
                    :, :, a * NARROW * BLOCK:(a + 1) * NARROW * BLOCK]
            return w3_tile(q)[:, BLOCK:BLOCK + 2 * row].rearrange("p (r n) -> p r n", r=2)[
                :, :, (2 * NARROW - 1) * BLOCK:]

        def unit_parts(u):
            p = unit_rows(u)
            if u < C2:
                return [(Q[0:p, u, :].rearrange("p (b e) -> p b e", e=BLOCK), 0, UW // BLOCK)]
            q, a = divmod(u - C2, W3_PARTS)
            if a < 2:
                return [(unit_read(u).rearrange("p r (b e) -> p r b e", e=BLOCK), 0, 2 * NARROW)]
            first = w3_tile(q)[:, 2 * NARROW * BLOCK:3 * NARROW * BLOCK]
            second = w3_tile(q)[:, PAIR - (NARROW + 1) * BLOCK:PAIR]
            return [(first.rearrange("p (b e) -> p b e", e=BLOCK), 0, NARROW),
                    (second.rearrange("p (b e) -> p b e", e=BLOCK), NARROW + 1, NARROW + 1)]

        def per_block(t, u, b, n):
            v = t[0:unit_rows(u), u % t.shape[1], b:b + n]
            return v.rearrange("p (r b) -> p r b", r=2) if n == 2 * NARROW else v

        def spread(t, u, b, n):
            v, p = per_block(t, u, b, n), unit_rows(u)
            if n == 2 * NARROW:
                return v.unsqueeze(3).broadcast_to([p, 2, NARROW, BLOCK])
            return v.unsqueeze(2).broadcast_to([p, n, BLOCK])

        def out_bank(q, t):
            return ((4, 5, 0, 1), (2, 3, 4, 5))[q][t // 2]

        @block.sync
        def _(sp):
            def load_job(j):
                kind, f = JOBS[j]
                if j >= RAW_SLOTS:
                    if j == RAW_SLOTS:
                        sp.wait_ge(s_wlo0, 1)
                    else:
                        sp.wait_ge(s_wlo, j - RAW_SLOTS)
                p, n = job_shape(j)
                src = {"pre": lambda: w_pre, "fuse": lambda: w_fuse[f], "in": lambda: w_in[:, f * 1024:f * 1024 + n],
                       "out": lambda: w_out[f * P:f * P + p, :]}[kind]()
                sp.dma_start(w_raw(j)[0:p, 0:n], src).then_inc(s_raw[j % RAW_SLOTS], 16)

            def load_unit(u):
                p = unit_rows(u)
                sp.dma_start(Q[0:p, u, 0:D], w1[u * P:u * P + p, :]).then_inc(s_q[u], 16)
                sp.dma_start(Q[0:p, u, D:2 * D], w2[u * P:u * P + p, :]).then_inc(s_q[u], 16)

            load_job(0)
            for c in range(DC):
                sp.dma_start(xT_raw[:, c, :], xT[:, c, :]).then_inc(s_x[c], 16)
            sp.dma_start(point_sb[:], point).then_inc(s_point, 16)
            sp.dma_start(disc[:], discount.broadcast_to([P, G])).then_inc(s_point, 16)
            load_unit(0)
            load_job(1)
            load_unit(1)
            for j in range(2, RAW_SLOTS):
                load_job(j)
            sp.dma_start(R[:], xN).then_inc(s_R, 16)
            sp.dma_start(ident[:], ident_in).then_inc(s_ident, 16)
            for u in range(2, C2):
                load_unit(u)
            for j in range(RAW_SLOTS, RAW_JOBS):
                load_job(j)
            sp.wait_ge(s_wlo, RAW_JOBS - 1)
            for q in range(2):
                sp.dma_start(w3_tile(q), w3[q * P:(q + 1) * P, :]).then_inc(s_w3[q], 16)
            for t in range(TT):
                sp.wait_ge(s_norm, TT + t + 1)
                sp.dma_start(out[t * P:(t + 1) * P, :], R[:, t, :]).then_inc(s_out, 16)
            sp.wait_ge(s_out, 16 * TT)

        @block.scalar
        def _(act):
            def copy(dst, src, **kw):
                return nc.scalar.activation(dst, src, ACT.Copy, **kw)

            def step_functions(key):
                a, b = PLAN[key]
                for s in range(a, b):
                    u, k = STEPS[s]
                    p, width = unit_rows(u), unit_width(u)
                    if k == 0:
                        act.wait_ge(s_nrm, normalised(u))
                        if u >= C2 and (u - C2) % W3_PARTS == 2:
                            act.wait_ge(s_dq, quantised(u - 2))
                    if s >= NR:
                        act.wait_ge(s_step, s - NR + 1)
                    dst = relu[0:p, s % NR, 0:width]
                    if u >= C2:
                        dst = dst.rearrange("p (r n) -> p r n", r=2)
                    nc.scalar.activation(dst, unit_read(u), ACT.Relu, scale=STEEP,
                                         bias=float(-BOUND[k]) * STEEP).then_inc(s_relu, 1)

            def split_raw(j):
                p, n = job_shape(j)
                act.wait_ge(s_raw[j % RAW_SLOTS], 16 * (j // RAW_SLOTS + 1))
                wait_w_slot(act, j)
                copy(w_slot(w_hi, j, p, n), w_raw(j)[0:p, 0:n]).then_inc(s_whi, 1)

            def split_h(job):
                kind, c = job
                p = job_rows(job)
                act.wait_ge(s_h, 2 * (c % C2 + 1) + (2 * C1 if kind == "nf4out" else 0))
                wait_h_slot(act, job)
                c %= C2
                copy(h_slots[job[1] % H_SLOTS][0][0:p, :], h[0:p, c * TOK:(c + 1) * TOK]).then_inc(s_lhi, 1)

            def silu(i, layer):
                f, half, g = i // 2, i % 2, i + (layer - 1) * 2 * C1
                p, bank = rows(f, F1 if layer == 1 else F2), pair_bank(layer, i)
                act.wait_ge(s_pair, g + 1)
                if layer == 2 and i == 0:
                    act.wait_ge(s_llo_h, sum(1 for kind, _ in GPSIMD_LO if kind == "out"))
                nc.scalar.activation(h[0:p, f * TOK + half * HALF:f * TOK + (half + 1) * HALF], PS[0:p, bank, :],
                                     ACT.Silu).then_inc(s_silu, 1)

            def root_of_variance(layer, group):
                act.wait_ge(s_ln, layer * len(NORM_GROUPS) + NORM_GROUPS.index(group) + 1)
                a, b = group[0], group[-1] + 1
                nc.scalar.activation(std[:, 1, a:b], std[:, 0, a:b], ACT.Sqrt).then_inc(s_sqrt, 1)

            for c in range(DC):
                if c == 0:
                    split_raw(0)
                act.wait_ge(s_x[c], 16)
                copy(x_hi[:, c, :], xT_raw[:, c, :]).then_inc(s_xh, 1)
            act.wait_ge(s_point, 32)
            nc.scalar.activation(fact[:], disc[:], ACT.Exp, scale=-1.0).then_inc(s_fact, 1)
            step_functions("start")
            act.wait_ge(s_fact, 1)
            for m in range(G + 1):
                split_raw(JOB["fuse", m])
                if m == 0:
                    act.wait_ge(s_pre, 2)
                    copy(l_hi[:, 0, :], PS[:, 0:2, :].rearrange("p b n -> p (b n)")).then_inc(s_lhi, 1)
                else:
                    act.wait_ge(s_t, m)
                    if m >= 2:
                        wait_stage2(act, m - 2)
                    copy(l_hi[:, m % 2, :], term_tile[m], scale=fact[:, m - 1:m]).then_inc(s_lhi, 1)
                step_functions(("term", m))
            split_raw(JOB["in", 0])
            for i in range(2 * C1):
                if i % 2 == 0:
                    split_raw(JOB["in", 0] + i // 2 + 1)
                step_functions(("pair", 1, i))
                silu(i, 1)
                if i % 2 == 1 and 1 <= i // 2 <= EARLY:
                    split_h(("out", i // 2 - 1))
            for f in range(C1):
                if f > 0:
                    split_raw(JOB["out", f])
                for c in range(EARLY, H_AHEAD) if f == 0 else []:
                    split_h(("out", c))
                if f + H_AHEAD < C1:
                    split_h(("out", f + H_AHEAD))
                if f < C1 - TAIL:
                    step_functions(("down", 1, f))
            for group in NORM_GROUPS:
                for t in group:
                    step_functions(("tile", t))
                root_of_variance(0, group)

            def split_nf4(f):
                j, m = JOB["nf4in", f], rows(f, F2)
                act.wait_ge(s_tr, f + 1)
                wait_w_slot(act, j)
                copy(w_slot(w_hi, j, P, 2 * DC * m).rearrange("p (c m) -> p c m", m=m),
                     PS[:, 6:8, :].rearrange("p b (c m) -> p (b c) m", m=P)[:, :, 0:m]).then_inc(s_whi, 1)

            for t in range(TT):
                if t == 6:
                    split_nf4(0)
                act.wait_ge(s_xtr, t + 1)
                copy(x_hi[:, :, t * P:(t + 1) * P],
                     PS[:, t % 6, :].rearrange("p (c t) -> p c t", c=DC)).then_inc(s_xh, 1)

            def split_w3(n):
                j, p = JOB["nf4out", n], rows(n % C2, F2)
                act.wait_ge(s_w3tr, n + 1)
                wait_w_slot(act, j)
                copy(w_slot(w_hi, j, p, 2 * P).rearrange("p (j r) -> p r j", r=2),
                     PS[0:p, 6 + n % 2, 0:2 * P].rearrange("p (r j) -> p r j", r=2)).then_inc(s_whi, 1)

            for i in range(2 * C2):
                step_functions(("pair", 2, i))
                if i == 2 * C2 - 1:
                    split_w3(0)
                silu(i, 2)
                if i % 2 == 0 and i // 2 + 1 < C2:
                    split_nf4(i // 2 + 1)
                if i % 2 == 1 and 1 <= i // 2 <= EARLY:
                    split_h(("nf4out", i // 2 - 1))
            for n in range(1, AHEAD):
                split_w3(n)
            for n in range(2 * C2):
                for c in range(EARLY, H_AHEAD) if n == 0 else []:
                    split_h(("nf4out", c))
                if n + H_AHEAD < 2 * C2:
                    split_h(("nf4out", n + H_AHEAD))
                step_functions(("down", 2, n))
                if n + AHEAD < 2 * C2:
                    split_w3(n + AHEAD)
            for group in NORM_GROUPS:
                root_of_variance(1, group)

        @block.vector
        def _(dve):
            v = nc.vector
            small = [0]

            def link(ins):
                small[0] += 1
                ins.then_inc(s_st, 1)
                dve.wait_ge(s_st, small[0])

            def scales(u):
                p, done = unit_rows(u), scaled(u - 1)
                if u < C2:
                    dve.wait_ge(s_q[u], 32)
                else:
                    dve.wait_ge(s_w3[(u - C2) // W3_PARTS], 16)
                parts = unit_parts(u)
                if u >= 4:
                    dve.wait_ge(s_dq, quantised(u - 4))
                for blocks, b, n in parts:
                    v.tensor_reduce(per_block(amax, u, b, n), blocks, AX_X, ALU.max,
                                    apply_absolute_value=True).then_inc(s_prep, 1)
                if u >= 2:
                    dve.wait_ge(s_nrm, normalised(u - 2))
                for i, (_, b, n) in enumerate(parts):
                    dve.wait_ge(s_prep, done + i + 1)
                    v.tensor_scalar(rcp[0:p, u % 2, b:b + n], amax[0:p, u % 4, b:b + n], TINY, None,
                                    ALU.max).then_inc(s_prep, 1)
                for i, (_, b, n) in enumerate(parts):
                    dve.wait_ge(s_prep, done + len(parts) + i + 1)
                    v.reciprocal(rcp[0:p, u % 2, b:b + n], rcp[0:p, u % 2, b:b + n]).then_inc(s_prep, 1)

            def add_steps(key):
                a, b = PLAN[key]
                for s in range(a, b):
                    for u in PREPS[s]:
                        scales(u)
                    u, k = STEPS[s]
                    p, width = unit_rows(u), unit_width(u)
                    sum_, step = acc[0:p, u % 2, 0:width], relu[0:p, s % NR, 0:width]
                    dve.wait_ge(s_relu, s + 1)
                    if k == 0:
                        if u >= 2:
                            dve.wait_ge(s_dq, quantised(u - 2))
                        v.tensor_scalar(sum_, step, RISE[0], float(CODE[0]), ALU.min, ALU.add).then_inc(s_step, 1)
                    else:
                        dve.wait_ge(s_step, STEPS.index((u, k - 1)) + 1)
                        v.scalar_tensor_tensor(sum_, step, RISE[k], sum_, ALU.min, ALU.add).then_inc(s_step, 1)

            def gate_times_up(i, layer):
                f, half, g = i // 2, i % 2, i + (layer - 1) * 2 * C1
                p, bank = rows(f, F1 if layer == 1 else F2), pair_bank(layer, i)
                hv = h[0:p, f * TOK + half * HALF:f * TOK + (half + 1) * HALF]
                dve.wait_ge(s_silu, g + 1)
                v.tensor_tensor(hv, PS[0:p, bank + 1, :], hv, ALU.mult).then_inc(s_h, 1)

            def add_tiles(n0, tiles):
                for t in tiles:
                    dve.wait_ge(s_tile, n0 + t + 1)
                    v.tensor_tensor(R[:, t, :], PS[:, t, :], R[:, t, :], ALU.add).then_inc(s_y, 1)

            def statistics(t, part, cols, added):
                dve.wait_ge(s_y, added)
                v.bn_stats(stats[:, t, part, :], R[:, t, cols]).then_inc(s_st, 1)
                small[0] += 1

            def normalise(group, parts, asked):
                a, b = group[0], group[-1] + 1
                dve.wait_ge(s_st, small[0])
                for t in group:
                    v.bn_aggr(mv[:, t, :], stats[:, t, 0:parts, :]).then_inc(s_st, 1)
                small[0] += len(group)
                dve.wait_ge(s_st, small[0])
                var, root, inv, tmp, tmp2 = (std[:, r, a:b] for r in range(5))
                v.tensor_scalar(var, mv[:, a:b, 1], EPS, None, ALU.add).then_inc(s_ln, 1)
                dve.wait_ge(s_sqrt, asked)
                link(v.reciprocal(inv, root))
                link(v.tensor_tensor(tmp, inv, inv, ALU.mult))
                link(v.scalar_tensor_tensor(tmp2, tmp, -0.5, var, ALU.mult, ALU.mult))
                link(v.scalar_tensor_tensor(tmp, tmp2, 1.5, inv, ALU.add, ALU.mult))
                for t in group:
                    v.tensor_scalar(R[:, t, :], R[:, t, :], mv[:, t, 0:1], std[:, 3, t:t + 1], ALU.subtract,
                                    ALU.mult).then_inc(s_norm, 1)

            p0, n0 = job_shape(0)
            dve.wait_ge(s_whi, 1)
            v.tensor_tensor(w_slot(w_lo, 0, p0, n0), w_raw(0)[0:p0, 0:n0], w_slot(w_hi, 0, p0, n0).bitcast(F32),
                            ALU.subtract).then_inc(s_wlo0, 1)
            for c in range(DC):
                dve.wait_ge(s_xh, c + 1)
                v.tensor_tensor(x_lo[:, c, :], xT_raw[:, c, :], x_hi[:, c, :].bitcast(F32),
                                ALU.subtract).then_inc(s_xl, 1)
            add_steps("start")
            dve.wait_ge(s_point, 32)
            dve.wait_ge(s_pre, 1)
            v.tensor_scalar(delta, PS[:, 2:4, :].rearrange("p b n -> p (b n)"), point_sb[:, 0:1], None,
                            ALU.subtract).then_inc(s_pre_read, 1)
            up = PS[:, 0:2, :].rearrange("p b n -> p (b n)")
            for m in range(G + 1):
                if m == 0:
                    dve.wait_ge(s_lhi, 1)
                    v.tensor_tensor(l_lo[:, 0, :], up, l_hi[:, 0, :].bitcast(F32), ALU.subtract).then_inc(s_llo_t, 1)
                    dve.wait_ge(s_pre_read, 1)
                    v.tensor_tensor(ta, up, delta, ALU.mult).then_inc(s_t, 1)
                    dve.wait_ge(s_t, 1)
                    v.scalar_tensor_tensor(kept, delta, THD, delta, ALU.is_le, ALU.mult).then_inc(s_keep, 1)
                    add_steps(("term", 0))
                    continue
                if m == 2:
                    dve.wait_ge(s_keep, 1)
                    v.scalar_tensor_tensor(kept, delta, -THD, kept, ALU.is_ge, ALU.mult).then_inc(s_keep, 1)
                if m < G:
                    dve.wait_ge(s_t, m)
                    if m >= 2:
                        dve.wait_ge(s_lhi, m)
                    if m + 1 == KEEP_FROM:
                        dve.wait_ge(s_keep, 2)
                    v.tensor_tensor(term_tile[m + 1], term_tile[m], kept if m + 1 == KEEP_FROM else delta,
                                    ALU.mult).then_inc(s_t, 1)
                dve.wait_ge(s_lhi, m + 1)
                if m == 1:
                    dve.wait_ge(s_fact, 1)
                if m >= 2:
                    wait_stage2(dve, m - 2)
                v.scalar_tensor_tensor(l_lo[:, m % 2, :], term_tile[m], fact[:, m - 1:m],
                                       l_hi[:, m % 2, :].bitcast(F32), ALU.mult, ALU.subtract).then_inc(s_llo_t, 1)
                add_steps(("term", m))
            dve.wait_ge(s_R, 16)
            add_tiles(0, range(TT))
            for i in range(2 * C1):
                add_steps(("pair", 1, i))
                gate_times_up(i, 1)
            for f in range(C1 - TAIL):
                add_steps(("down", 1, f))
                if ("out", f + H_AHEAD) in VECTOR_LO:
                    lo_of_h(dve, v, ("out", f + H_AHEAD), s_llo_v)
            dve.wait_ge(s_y, TT)
            for g_, group in enumerate(NORM_GROUPS):
                for t in group:
                    add_steps(("tile", t))
                    add_tiles(TT, [t])
                    statistics(t, 0, slice(0, D), TT + t + 1)
                normalise(group, 1, g_ + 1)

            def lo_nf4(f):
                j, m = JOB["nf4in", f], rows(f, F2)
                n = 2 * DC * m
                dve.wait_ge(s_whi, j + 1)
                wait_w_slot(dve, j)
                v.tensor_tensor(w_slot(w_lo, j, P, n).rearrange("p (c m) -> p c m", m=m),
                                PS[:, 6:8, :].rearrange("p b (c m) -> p (b c) m", m=P)[:, :, 0:m],
                                w_slot(w_hi, j, P, n).bitcast(F32).rearrange("p (c m) -> p c m", m=m),
                                ALU.subtract).then_inc(s_wlo4, 1)

            for t in range(TT):
                if t == 6:
                    lo_nf4(0)
                dve.wait_ge(s_xh, DC + t + 1)
                v.tensor_tensor(x_lo[:, :, t * P:(t + 1) * P],
                                PS[:, t % 6, :].rearrange("p (c t) -> p c t", c=DC),
                                x_hi[:, :, t * P:(t + 1) * P].bitcast(F32), ALU.subtract).then_inc(s_xl, 1)

            def lo_w3(n):
                j, p = JOB["nf4out", n], rows(n % C2, F2)
                dve.wait_ge(s_whi, j + 1)
                wait_w_slot(dve, j)
                v.tensor_tensor(w_slot(w_lo, j, p, 2 * P).rearrange("p (j r) -> p r j", r=2),
                                PS[0:p, 6 + n % 2, 0:2 * P].rearrange("p (r j) -> p r j", r=2),
                                w_slot(w_hi, j, p, 2 * P).bitcast(F32).rearrange("p (j r) -> p r j", r=2),
                                ALU.subtract).then_inc(s_wlo4, 1)

            for i in range(2 * C2):
                add_steps(("pair", 2, i))
                if i == 2 * C2 - 1:
                    lo_w3(0)
                gate_times_up(i, 2)
                if i % 2 == 0 and i // 2 + 1 < C2:
                    lo_nf4(i // 2 + 1)
            for n in range(1, AHEAD):
                lo_w3(n)

            def add_columns(q, b):
                cols = slice(q * 2 * P, (q + 1) * 2 * P)
                dve.wait_ge(s_tile, TT * (2 + q) + 2 * b + 2)
                rv = R[:, 2 * b:2 * b + 2, cols]
                v.tensor_tensor(rv, PS[:, out_bank(q, 2 * b), :].rearrange("p (t n) -> p t n", t=2), rv,
                                ALU.add).then_inc(s_y, 1)

            for n in range(2 * C2):
                if n == C2:
                    for b in range(TT // 2):
                        add_columns(0, b)
                add_steps(("down", 2, n))
                if n + AHEAD < 2 * C2:
                    lo_w3(n + AHEAD)
                if C2 < n <= C2 + TT // 2:
                    for t in (2 * (n - C2 - 1), 2 * (n - C2 - 1) + 1):
                        statistics(t, 0, slice(0, 2 * P), 2 * TT + t // 2 + 1)
            for g_, group in enumerate(NORM_GROUPS):
                for b in range(group[0] // 2, group[-1] // 2 + 1):
                    add_columns(1, b)
                    for t in (2 * b, 2 * b + 1):
                        statistics(t, 1, slice(2 * P, 4 * P), 2 * TT + TT // 2 + b + 1)
                normalise(group, 2, len(NORM_GROUPS) + g_ + 1)

        @block.gpsimd
        def _(pool):
            g = nc.gpsimd

            def scale_units(key):
                a, b = PLAN[key]
                for s in range(a, b):
                    for u in PREPS[s]:
                        pool.wait_ge(s_prep, scaled(u))
                        for blocks, b0, n in unit_parts(u):
                            g.tensor_tensor(blocks, blocks, spread(rcp, u, b0, n), ALU.mult).then_inc(s_nrm, 1)
                    u, k = STEPS[s]
                    if k == NB - 1:
                        pool.wait_ge(s_step, s + 1)
                        for blocks, b0, n in unit_parts(u):
                            codes = acc[0:unit_rows(u), u % 2, b0 * BLOCK:(b0 + n) * BLOCK]
                            codes = (codes.rearrange("p (r b e) -> p r b e", r=2, e=BLOCK) if n == 2 * NARROW
                                     else codes.rearrange("p (b e) -> p b e", e=BLOCK))
                            g.tensor_tensor(blocks, codes, spread(amax, u, b0, n), ALU.mult).then_inc(s_dq, 1)

            def lo_raw(j):
                p, n = job_shape(j)
                pool.wait_ge(s_whi, j + 1)
                wait_w_slot(pool, j)
                g.tensor_tensor(w_slot(w_lo, j, p, n), w_raw(j)[0:p, 0:n], w_slot(w_hi, j, p, n).bitcast(F32),
                                ALU.subtract).then_inc(s_wlo, 1)

            scale_units("start")
            for m in range(G + 1):
                lo_raw(JOB["fuse", m])
                scale_units(("term", m))
            lo_raw(JOB["in", 0])
            for i in range(2 * C1):
                if i % 2 == 0:
                    lo_raw(JOB["in", 0] + i // 2 + 1)
                scale_units(("pair", 1, i))
                if i % 2 == 1 and 1 <= i // 2 <= EARLY:
                    lo_of_h(pool, g, ("out", i // 2 - 1), s_llo_h)
            for f in range(C1):
                if f > 0:
                    lo_raw(JOB["out", f])
                for c in range(EARLY, H_AHEAD + 1) if f == 0 else [f + H_AHEAD]:
                    if ("out", c) in GPSIMD_LO:
                        lo_of_h(pool, g, ("out", c), s_llo_h)
                if f < C1 - TAIL:
                    scale_units(("down", 1, f))
            for t in range(TT):
                scale_units(("tile", t))
            for i in range(2 * C2):
                scale_units(("pair", 2, i))
                if i % 2 == 1 and 1 <= i // 2 <= EARLY:
                    lo_of_h(pool, g, ("nf4out", i // 2 - 1), s_llo_h)
            for n in range(2 * C2):
                for c in range(EARLY, H_AHEAD + 1) if n == 0 else [n + H_AHEAD]:
                    if ("nf4out", c) in GPSIMD_LO:
                        lo_of_h(pool, g, ("nf4out", c), s_llo_h)
                scale_units(("down", 2, n))

        @block.tensor
        def _(pe):
            t_ = nc.tensor

            def product(dst, a_hi, a_lo, b_hi, b_lo, start, stop, shared=False):
                t_.matmul(dst, a_hi, b_hi, start=start, stop=False, skip_group_check=shared)
                t_.matmul(dst, a_hi, b_lo, start=False, stop=False, skip_group_check=shared)
                return t_.matmul(dst, a_lo, b_hi, start=False, stop=stop, skip_group_check=shared)

            def wait_job(j):
                kind, f = JOBS[j]
                pe.wait_ge(s_whi, j + 1)
                if kind in ("nf4in", "nf4out"):
                    pe.wait_ge(s_wlo4, f + 1 + (C2 if kind == "nf4out" else 0))
                elif j == 0:
                    pe.wait_ge(s_wlo0, 1)
                else:
                    pe.wait_ge(s_wlo, j)

            def project(j, kind, half, bank, m):
                wh = w_hi[:, j % 2, 0:2 * DC * m].rearrange("p (g c m) -> p g c m", g=2, c=DC)
                wl = w_lo[:, j % 2, 0:2 * DC * m].rearrange("p (g c m) -> p g c m", g=2, c=DC)
                for c in range(DC):
                    xs = slice(half * HALF, (half + 1) * HALF)
                    last = product(PS[0:m, bank, :], wh[:, kind, c, :], wl[:, kind, c, :], x_hi[:, c, xs],
                                   x_lo[:, c, xs], c == 0, c == DC - 1)
                return last

            def pair(i, layer, job):
                f, half, m = i // 2, i % 2, rows(i // 2, F1 if layer == 1 else F2)
                bank = pair_bank(layer, i)
                if half == 0:
                    wait_job(job)
                if i >= 3:
                    pe.wait_ge(s_h, i - 2 + (layer - 1) * 2 * C1)
                elif layer == 1:
                    pe.wait_ge(s_y, bank + 2)
                else:
                    pe.wait_ge(s_xl, DC + (4 if i == 0 else TT))
                project(job, 0, half, bank, m)
                last = project(job, 1, half, bank + 1, m)
                last.then_inc(s_pair, 1)

            def operands(job):
                kind, f = job
                j, p = JOB[job], job_rows(job)
                wait_job(j)
                if kind == "fuse":
                    pe.wait_ge(s_lhi, f + 1)
                    pe.wait_ge(s_llo_t, f + 1)
                    hi, lo = l_hi[:, f % 2, :], l_lo[:, f % 2, :]
                else:
                    if job in VECTOR_LO:
                        pe.wait_ge(s_llo_v, VECTOR_LO.index(job) + 1)
                    else:
                        pe.wait_ge(s_llo_h, GPSIMD_LO.index(job) + 1)
                    hi, lo = (x[0:p, :] for x in h_slots[f % H_SLOTS])
                width = 2 * P if kind == "nf4out" else D
                return hi, lo, w_slot(w_hi, j, p, width), w_slot(w_lo, j, p, width)

            def stage2_tile(job, ops, t, first, last):
                hi, lo, wh, wl = ops
                kind, f = job
                ts = slice(t * P, (t + 1) * P)
                if kind != "nf4out":
                    return product(PS[:, t, :], hi[:, ts], lo[:, ts], wh, wl, first, last)
                dst = PS[:, out_bank(f // C2, t), (t % 2) * 2 * P:(t % 2 + 1) * 2 * P]
                return product(dst, hi[:, ts], lo[:, ts], wh, wl, first and t % 2 == 0, last, True)

            def stage2(job, first=False, last=False, order=range(TT), wait={}):
                ops = operands(job)
                for t in order:
                    if t in wait:
                        pe.wait_ge(*wait[t])
                    ins = stage2_tile(job, ops, t, first, last)
                    if last:
                        ins.then_inc(s_tile, 1)
                    elif t == order[-1]:
                        ins.then_inc(s_l_used, 1)

            def stage2_end(jobs, t, ops):
                for job, o in zip(jobs, ops):
                    ins = stage2_tile(job, o, t, False, job == jobs[-1])
                ins.then_inc(s_tile, 1)

            def transpose_nf4(f):
                m = rows(f, F2)
                pe.wait_ge(s_dq, quantised(f))
                if f >= 1:
                    pe.wait_ge(s_wlo4, f)
                for g_ in range(2):
                    for c in range(DC):
                        last = t_.transpose(PS[:, 6 + g_, c * P:c * P + m],
                                            Q[0:m, f, g_ * D + c * P:g_ * D + (c + 1) * P], ident[0:m, 0:m])
                last.then_inc(s_tr, 1)

            wait_job(0)
            wh0 = w_hi[:, 0, :].rearrange("p (g c m) -> p g c m", g=2, c=DC)
            wl0 = w_lo[:, 0, :].rearrange("p (g c m) -> p g c m", g=2, c=DC)
            for c in range(DC):
                pe.wait_ge(s_xh, c + 1)
                pe.wait_ge(s_xl, c + 1)
                for kind in (1, 0):
                    for half in range(2):
                        xs = slice(half * HALF, (half + 1) * HALF)
                        last = product(PS[:, 2 * kind + half, :], wh0[:, kind, c, :], wl0[:, kind, c, :],
                                       x_hi[:, c, xs], x_lo[:, c, xs], c == 0, c == DC - 1)
                    if c == DC - 1:
                        last.then_inc(s_pre, 1)
            for m in range(G + 1):
                if m == 0:
                    stage2(("fuse", 0), first=True, order=[4, 5, 6, 7, 2, 3, 0, 1],
                           wait={2: (s_pre_read, 1), 0: (s_t, 1)})
                else:
                    stage2(("fuse", m), last=m == G)
            for i in range(2 * C1):
                pair(i, 1, JOB["in", i // 2])
            order, wait = [6, 7], {}
            for i in range(2 * C1 - 3, 2 * C1):
                bank = pair_bank(1, i)
                order += [bank, bank + 1]
                wait[bank] = (s_h, i + 1)
            for f in range(C1 - TAIL):
                if f == 0:
                    stage2(("out", 0), first=True, order=order, wait=wait)
                else:
                    stage2(("out", f))

            def transpose_x(t):
                pe.wait_ge(s_norm, t + 1)
                if t >= 6:
                    pe.wait_ge(s_xl, DC + t - 5)
                for c in range(DC):
                    last = t_.transpose(PS[:, t % 6, c * P:(c + 1) * P], R[:, t, c * P:(c + 1) * P], ident[:])
                last.then_inc(s_xtr, 1)

            jobs = [("out", f) for f in range(C1 - TAIL, C1)]
            ops = [operands(job) for job in jobs]
            pe.wait_ge(s_ident, 16)
            for t in range(TT):
                stage2_end(jobs, t, ops)
                if t == 6:
                    transpose_x(0)
                    transpose_x(1)
            for t in range(2, 6):
                transpose_x(t)
            pe.wait_ge(s_y, 2 * TT)
            transpose_nf4(0)
            transpose_x(6)
            transpose_x(7)

            def transpose_w3(n):
                q, c = divmod(n, C2)
                m = rows(c, F2)
                pe.wait_ge(s_dq, quantised(w3_unit_of(q, c)))
                pe.wait_ge(s_wlo4, C2 + (n - 1 if n >= 2 else 0))
                for r in range(2):
                    last = t_.transpose(PS[0:m, 6 + n % 2, r * P:(r + 1) * P],
                                        w3_tile(q)[:, r * F2 + c * P:r * F2 + c * P + m], ident[:])
                last.then_inc(s_w3tr, 1)

            for i in range(2 * C2):
                pair(i, 2, JOB["nf4in", i // 2])
                if i % 2 == 0 and i // 2 + 1 < C2:
                    transpose_nf4(i // 2 + 1)
                if i == 2 * C2 - 2:
                    for n in range(2):
                        transpose_w3(n)
            for n in range(2, AHEAD):
                transpose_w3(n)
            jobs = [("nf4out", n) for n in range(2 * C2 - TAIL, 2 * C2)]
            for n in range(2 * C2 - TAIL):
                if n == 0:
                    wait = {0: (s_h, 2 * C1 + 2 * C2 - 2), 4: (s_h, 2 * C1 + 2 * C2 - 1)}
                elif n == C2:
                    wait = {0: (s_h, 2 * C1 + 2 * C2), 4: (s_y, 2 * TT + 1), 6: (s_y, 2 * TT + 2)}
                stage2(("nf4out", n), first=n % C2 == 0, last=n == C2 - 1, wait=wait if n % C2 == 0 else {})
                if n + AHEAD < 2 * C2:
                    transpose_w3(n + AHEAD)
            for n in range(2 * C2 - TAIL + AHEAD, 2 * C2):
                transpose_w3(n)
            ops = [operands(job) for job in jobs]
            for t in range(TT):
                stage2_end(jobs, t, ops)


def kernel(L0_attn_hidden_states, L0_attn_up_w, L0_attn_gate_w, L0_attn_local_point, L0_attn_local_approx_output,
           L0_attn_fuse_weight, L0_attn_discount_factor, L0_attn_ffn_gate_w, L0_attn_ffn_up_w, L0_attn_ffn_down_w,
           L0_ffn_w1, L0_ffn_w2, L0_ffn_w3):
    import concourse.bacc as bacc
    from concourse.bass_utils import run_bass_kernel_spmd

    def a(t):
        return np.asarray(t)

    def chunks_in(*ws):
        width = ws[0].shape[0]
        parts = []
        for f in range(-(-width // P)):
            m = min(P, width - f * P)
            both = np.stack([w[f * P:f * P + m].reshape(m, DC, P) for w in ws])
            parts.append(both.transpose(3, 0, 2, 1).reshape(P, 2 * DC * m))
        return np.ascontiguousarray(np.concatenate(parts, axis=1))

    x = a(L0_attn_hidden_states)
    x2 = x.reshape(TOK, D)
    fuse = a(L0_attn_fuse_weight)
    arrays = {
        "xT": np.ascontiguousarray(x2.T.reshape(DC, P, TOK).transpose(1, 0, 2)),
        "xN": np.ascontiguousarray(x2.reshape(TT, P, D).transpose(1, 0, 2)),
        "w_pre": chunks_in(a(L0_attn_up_w), a(L0_attn_gate_w)),
        "w_fuse": np.ascontiguousarray(np.stack([a(L0_attn_local_approx_output).T]
                                                + [fuse[:, :, g].T for g in range(G)])),
        "w_in": chunks_in(a(L0_attn_ffn_gate_w), a(L0_attn_ffn_up_w)),
        "w_out": np.ascontiguousarray(a(L0_attn_ffn_down_w).T),
        "point": a(L0_attn_local_point).reshape(S, 1),
        "discount": a(L0_attn_discount_factor).reshape(1, G),
        "w1": np.ascontiguousarray(a(L0_ffn_w1)),
        "w2": np.ascontiguousarray(a(L0_ffn_w2)),
        "w3": np.ascontiguousarray(a(L0_ffn_w3)).reshape(D // 2, PAIR),
        "ident_in": np.eye(P, dtype=np.float32),
    }
    nc = bacc.Bacc("TRN2", target_bir_lowering=False, num_devices=1)
    args = {name: nc.dram_tensor(name, v.shape, mybir.dt.from_np(v.dtype), kind="ExternalInput").ap()
            for name, v in arrays.items()}
    out = nc.dram_tensor("out", (TOK, D), F32, kind="ExternalOutput").ap()
    build(nc, **args, out=out)
    r = run_bass_kernel_spmd(nc, [arrays], core_ids=[0])
    return r.results[0]["out"].reshape(x.shape)
```
